# Optimizing a Trainium2 kernel written in Bass

```python
import numpy as np
import jax
import jax.numpy as jnp

def _softmax(x, axis=-1):
    return jax.nn.softmax(x, axis=axis)

def _gelu(x):
    return jax.nn.gelu(x, approximate=True)

def _silu(x):
    return jax.nn.silu(x)

def _sigmoid(x):
    return jax.nn.sigmoid(x)

def _layernorm(x, axis=-1, eps=1e-05):
    m = jnp.mean(x, axis=axis, keepdims=True)
    v = jnp.var(x, axis=axis, keepdims=True)
    return (x - m) / jnp.sqrt(v + eps)

def _scatter_add(tgt, idx, src, axis=0):
    return tgt.at[idx].add(src)

def _segment_sum(src, seg, n):
    return jax.ops.segment_sum(src, seg, n)
kernel_name = 'mk_macaron_d1_jaxref_r4_f3aa52'

def setup_inputs(seed: int=0):
    np.random.seed(seed)
    _w = jnp.asarray

    def _L0_attn_setup():
        import jax, jax.numpy as jnp
        import numpy as np
        DIM = 256
        NUM_HEADS = 16
        HD = DIM // NUM_HEADS
        ROPE_DIM = 64
        ROPE_BASE = 10000.0

        def _apply_rope(t):
            D = t.shape[-1]
            N = t.shape[2]
            pos = jnp.arange(N, dtype=t.dtype)
            inv = 1.0 / ROPE_BASE ** (jnp.arange(0, D, 2, dtype=t.dtype) / D)
            freqs = pos[:, None] * inv[None, :]
            cos = jnp.cos(freqs)[None, None]
            sin = jnp.sin(freqs)[None, None]
            e = t[..., 0::2]
            o = t[..., 1::2]
            eo = e * cos - o * sin
            oo = e * sin + o * cos
            return jnp.stack([eo, oo], axis=-1).reshape(t.shape)
        key = jax.random.key(seed)
        ks = jax.random.split(key, 5)
        B, N = (2, 512)
        s = 0.02
        return {'x': jax.random.normal(ks[0], (B, N, DIM), dtype=jnp.float32), 'qkv_w': jax.random.normal(ks[1], (3 * DIM, DIM), dtype=jnp.float32) * s, 'qkv_b': jax.random.normal(ks[2], (3 * DIM,), dtype=jnp.float32) * s, 'proj_w': jax.random.normal(ks[3], (DIM, DIM), dtype=jnp.float32) * s, 'proj_b': jax.random.normal(ks[4], (DIM,), dtype=jnp.float32) * s}
    _L0_attn_in = _L0_attn_setup()

    def _L0_ffn_setup():
        import jax, jax.numpy as jnp
        import numpy as np
        DIM = 256

        def _reference_tuple_inner(x, W_r, W_k, W_v, mu_r, mu_k):
            B, T, C = x.shape
            x_prev = jnp.concatenate([jnp.zeros((B, 1, C), x.dtype), x[:, :-1, :]], axis=1)
            xr = mu_r * x + (1.0 - mu_r) * x_prev
            xk = mu_k * x + (1.0 - mu_k) * x_prev
            r = jax.nn.sigmoid(jnp.einsum('btc,dc->btd', xr, W_r))
            k = jnp.einsum('btc,dc->btd', xk, W_k)
            k_act = jnp.square(jax.nn.relu(k))
            out = r * jnp.einsum('btc,dc->btd', k_act, W_v)
            new_state = x[:, -1, :]
            return (out, new_state)
        key = jax.random.key(seed)
        ks = jax.random.split(key, 6)
        B, T, C = (8, 512, DIM)
        x = jax.random.normal(ks[0], (B, T, C), dtype=jnp.float32)
        s = 1.0 / np.sqrt(C)
        W_r = jax.random.uniform(ks[1], (C, C), jnp.float32, -s, s)
        W_k = jax.random.uniform(ks[2], (C, C), jnp.float32, -s, s)
        W_v = jax.random.uniform(ks[3], (C, C), jnp.float32, -s, s)
        mu_r = jax.random.uniform(ks[4], (C,), jnp.float32)
        mu_k = jax.random.uniform(ks[5], (C,), jnp.float32)
        return {'x': x, 'W_r': W_r, 'W_k': W_k, 'W_v': W_v, 'mu_r': mu_r, 'mu_k': mu_k}
    _L0_ffn_in = _L0_ffn_setup()
    _d = {'L0_attn_x': _L0_attn_in['x'], 'L0_attn_qkv_w': _L0_attn_in['qkv_w'], 'L0_attn_qkv_b': _L0_attn_in['qkv_b'], 'L0_attn_proj_w': _L0_attn_in['proj_w'], 'L0_attn_proj_b': _L0_attn_in['proj_b'], 'L0_ffn_W_r': _L0_ffn_in['W_r'], 'L0_ffn_W_k': _L0_ffn_in['W_k'], 'L0_ffn_W_v': _L0_ffn_in['W_v'], 'L0_ffn_mu_r': _L0_ffn_in['mu_r'], 'L0_ffn_mu_k': _L0_ffn_in['mu_k']}
    _x0 = _d['L0_attn_x']
    _d['L0_attn_x'] = jax.random.normal(jax.random.fold_in(jax.random.key(seed), 1), (4, 2048, 256), dtype=_x0.dtype)
    del _x0
    return _d

def reference(L0_attn_x, L0_attn_qkv_w, L0_attn_qkv_b, L0_attn_proj_w, L0_attn_proj_b, L0_ffn_W_r, L0_ffn_W_k, L0_ffn_W_v, L0_ffn_mu_r, L0_ffn_mu_k):

    def _L0_attn_ref(x, qkv_w, qkv_b, proj_w, proj_b):
        import jax, jax.numpy as jnp
        import numpy as np
        DIM = 256
        NUM_HEADS = 16
        HD = DIM // NUM_HEADS
        ROPE_DIM = 64
        ROPE_BASE = 10000.0

        def _apply_rope(t):
            D = t.shape[-1]
            N = t.shape[2]
            pos = jnp.arange(N, dtype=t.dtype)
            inv = 1.0 / ROPE_BASE ** (jnp.arange(0, D, 2, dtype=t.dtype) / D)
            freqs = pos[:, None] * inv[None, :]
            cos = jnp.cos(freqs)[None, None]
            sin = jnp.sin(freqs)[None, None]
            e = t[..., 0::2]
            o = t[..., 1::2]
            eo = e * cos - o * sin
            oo = e * sin + o * cos
            return jnp.stack([eo, oo], axis=-1).reshape(t.shape)
        B, N, C = x.shape
        H, D = (NUM_HEADS, HD)
        scale = D ** (-0.5)
        qkv = x @ qkv_w.T + qkv_b
        qkv = qkv.reshape(B, N, 3, H, D).transpose(2, 0, 3, 1, 4)
        q, k, v = (qkv[0], qkv[1], qkv[2])
        q = jnp.concatenate([_apply_rope(q[..., :ROPE_DIM]), q[..., ROPE_DIM:]], axis=-1)
        k = jnp.concatenate([_apply_rope(k[..., :ROPE_DIM]), k[..., ROPE_DIM:]], axis=-1)
        attn = jnp.einsum('bhnd,bhmd->bhnm', q, k) * scale
        attn = jax.nn.softmax(attn, axis=-1)
        out = jnp.einsum('bhnm,bhmd->bhnd', attn, v)
        out = out.transpose(0, 2, 1, 3).reshape(B, N, C)
        return out @ proj_w.T + proj_b

    def _L0_ffn_ref(x, W_r, W_k, W_v, mu_r, mu_k):
        import jax, jax.numpy as jnp
        import numpy as np
        DIM = 256

        def _reference_tuple_inner(x, W_r, W_k, W_v, mu_r, mu_k):
            B, T, C = x.shape
            x_prev = jnp.concatenate([jnp.zeros((B, 1, C), x.dtype), x[:, :-1, :]], axis=1)
            xr = mu_r * x + (1.0 - mu_r) * x_prev
            xk = mu_k * x + (1.0 - mu_k) * x_prev
            r = jax.nn.sigmoid(jnp.einsum('btc,dc->btd', xr, W_r))
            k = jnp.einsum('btc,dc->btd', xk, W_k)
            k_act = jnp.square(jax.nn.relu(k))
            out = r * jnp.einsum('btc,dc->btd', k_act, W_v)
            new_state = x[:, -1, :]
            return (out, new_state)
        return _reference_tuple_inner(x, W_r, W_k, W_v, mu_r, mu_k)[0]
    x = L0_attn_x
    x = x + 0.5 * _L0_ffn_ref(_layernorm(x, axis=-1), L0_ffn_W_r, L0_ffn_W_k, L0_ffn_W_v, L0_ffn_mu_r, L0_ffn_mu_k)
    x = x + _L0_attn_ref(_layernorm(x, axis=-1), L0_attn_qkv_w, L0_attn_qkv_b, L0_attn_proj_w, L0_attn_proj_b)
    x = x + 0.5 * _L0_ffn_ref(_layernorm(x, axis=-1), L0_ffn_W_r, L0_ffn_W_k, L0_ffn_W_v, L0_ffn_mu_r, L0_ffn_mu_k)
    return x

_drawn_inputs = setup_inputs


def setup_inputs(seed=0):
    import zlib

    import numpy as np

    out = dict(_drawn_inputs(seed))
    spreads = {}
    factors = {'L0_attn_qkv_w': 8.0,
     'L0_attn_qkv_b': 7.488,
     'L0_attn_proj_w': 7.992,
     'L0_attn_proj_b': 14.923,
     'L0_ffn_W_r': 3.173,
     'L0_ffn_mu_r': 6.387}
    for name, (base, spread) in spreads.items():
        noise = np.random.default_rng([zlib.crc32(name.encode()), seed]).standard_normal(out[name].shape)
        drawn = base * np.exp(spread * noise) if base else spread * noise
        out[name] = jnp.asarray(drawn.astype(out[name].dtype))
    for name, factor in factors.items():
        out[name] = (out[name] * factor).astype(out[name].dtype)
    return out
```

```python
from contextlib import ExitStack

import concourse.bass as bass
from concourse import mybir

F32 = mybir.dt.float32
BF16 = mybir.dt.bfloat16
I32 = mybir.dt.int32
ALU = mybir.AluOpType
ACT = mybir.ActivationFunctionType
AX = mybir.AxisListType

P = 128
EPS = 1e-5
PARTS = 3
PAIRS = [(0, 0), (0, 1), (0, 2), (1, 0), (1, 1), (2, 0)]


def after(eng, sem, count):
    if isinstance(count, int) and count <= 0:
        return
    eng.wait_ge(sem, count)


def snap(eng, value):
    return value if isinstance(value, int) else eng.snap(eng.to_reg(value))


def looped(eng, n, step):
    step(0)
    with eng.Fori(1, n - 1) as i:
        step(i)
    step(n - 1)


def macaron(nc, x, wr_t, wk_t, wv_t, mu_r, mu_k, qkv_t, qk_b, qkv_b, proj_t, proj_b, cos, sin, out):
    B, N, C = x.shape
    H, D = 16, C // 16
    T = B * N // P
    GT = 4
    W = GT * P
    G = T // GT
    GB = G // B
    CC = C // P
    TB = T // B
    HEADS = B * H
    R = len(PAIRS) * D
    NJ = N // W
    scale = float(D) ** -0.5

    x_tiles = x.rearrange("b (t p) c -> p (b t) c", p=P)
    out_tiles = out.rearrange("b (t p) c -> p (b t) c", p=P)
    split_dram = nc.dram_tensor("split_dram", (2, PARTS, C, B * N), BF16, kind="Internal").ap()

    ctx = ExitStack()
    with ctx:
        def sb(name, shape, dt, on=ctx):
            return on.enter_context(nc.sbuf_tensor(name, shape, dt))

        def ps(name, shape, dt, on):
            return on.enter_context(nc.psum_tensor(name, shape, dt))

        def sem(name, on):
            return on.enter_context(nc.semaphore(name))

        x_all = sb("x_all", [P, T, C], F32)
        ident = sb("ident", [P, P], F32)
        ident_b = sb("ident_b", [P, P], BF16)
        w_r = sb("w_r", [P, CC, C], F32)
        w_k = sb("w_k", [P, CC, C], F32)
        w_v = sb("w_v", [P, CC, C], F32)
        w_qkv = sb("w_qkv", [P, CC, 3 * C], F32)
        w_proj = sb("w_proj", [P, CC, C], F32)
        mu_rt = sb("mu_rt", [P, CC], F32)
        mu_kt = sb("mu_kt", [P, CC], F32)
        b_qk = sb("b_qk", [P, 2 * CC], F32)
        b_v = sb("b_v", [P, C], F32)
        b_proj = sb("b_proj", [P, C], F32)
        stats = sb("stats", [P, T, 6], F32)
        rstd = sb("rstd", [P, T], F32)
        shift = sb("shift", [P, T], F32)

        def ln_scalars(name):
            with ExitStack() as on:
                half = sb(f"{name}_half", [P, T], F32, on)
                mean = sb(f"{name}_mean", [P, T], F32, on)
                var = sb(f"{name}_var", [P, T], F32, on)
                root = sb(f"{name}_root", [P, T], F32, on)
                var_ready = sem(f"{name}_var_ready", on)
                root_ready = sem(f"{name}_root_ready", on)
                chain = sem(f"{name}_chain", on)
                with nc.Block() as block:
                    @block.vector
                    def _(dve):
                        done = [0]

                        def link(ins):
                            done[0] += 1
                            ins.then_inc(chain, 1)
                            dve.wait_ge(chain, done[0])

                        even, odd = stats[:, :, 1], stats[:, :, 4]
                        dve.tensor_tensor(half[:], even, odd, ALU.subtract).then_inc(chain, 1)
                        dve.tensor_tensor(mean[:], even, odd, ALU.add).then_inc(chain, 1)
                        dve.tensor_tensor(var[:], stats[:, :, 2], stats[:, :, 5], ALU.add).then_inc(chain, 1)
                        done[0] = 3
                        dve.wait_ge(chain, 3)
                        link(dve.scalar_tensor_tensor(out=half[:], in0=half[:], scalar=0.25, in1=half[:],
                                                      op0=ALU.mult, op1=ALU.mult))
                        link(dve.scalar_tensor_tensor(out=var[:], in0=var[:], scalar=1.0 / C, in1=half[:],
                                                      op0=ALU.mult, op1=ALU.add))
                        dve.tensor_scalar(var[:], var[:], EPS, None, ALU.add).then_inc(var_ready, 1)
                        dve.wait_ge(root_ready, 1)
                        link(dve.reciprocal(rstd[:], root[:]))
                        link(dve.tensor_tensor(half[:], rstd[:], rstd[:], ALU.mult))
                        link(dve.tensor_tensor(half[:], half[:], var[:], ALU.mult))
                        link(dve.tensor_scalar(half[:], half[:], -0.5, 1.5, ALU.mult, ALU.add))
                        link(dve.tensor_tensor(rstd[:], rstd[:], half[:], ALU.mult))
                        link(dve.scalar_tensor_tensor(out=shift[:], in0=mean[:], scalar=-0.5, in1=rstd[:],
                                                      op0=ALU.mult, op1=ALU.mult))

                    @block.scalar
                    def _(act):
                        act.wait_ge(var_ready, 1)
                        act.activation(root[:], var[:], ACT.Sqrt).then_inc(root_ready, 1)

        with ExitStack() as on:
            x_loaded = [sem(f"x_loaded{b}", on) for b in range(B)]
            w_loaded = sem("w_loaded", on)
            zeroed = sem("zeroed", on)
            ident_ready = sem("ident_ready", on)
            stats_ready = sem("stats_ready", on)
            n_w = 12
            with nc.Block() as block:
                @block.sync
                def _(sp):
                    for b in range(B):
                        sp.dma_start(x_all[:, b * TB:(b + 1) * TB, :],
                                     x_tiles[:, b * TB:(b + 1) * TB, :]).then_inc(x_loaded[b], 16)

                @block.scalar
                def _(act):
                    chunked = "(c p) n -> p c n"
                    for dst, src in ((w_r, wr_t), (w_k, wk_t), (w_v, wv_t), (w_qkv, qkv_t), (w_proj, proj_t)):
                        act.dma_start(dst[:], src.rearrange(chunked, p=P)).then_inc(w_loaded, 16)
                    act.dma_start(mu_rt[:], mu_r).then_inc(w_loaded, 16)
                    act.dma_start(mu_kt[:], mu_k).then_inc(w_loaded, 16)
                    act.dma_start(b_qk[:], qk_b).then_inc(w_loaded, 16)
                    act.dma_start(b_v[:], qkv_b[2 * C:3 * C].rearrange("(o n) -> o n", o=1)
                                  .broadcast_to([P, C])).then_inc(w_loaded, 16)
                    act.dma_start(b_proj[:], proj_b.rearrange("(o n) -> o n", o=1)
                                  .broadcast_to([P, C])).then_inc(w_loaded, 16)
                    act.wait_ge(w_loaded, 16 * 10)

                @block.gpsimd
                def _(pool):
                    pool.memset(ident[:], 0.0).then_inc(zeroed, 1)
                    pool.memset(ident_b[:], 0.0).then_inc(zeroed, 1)
                    pool.wait_ge(zeroed, 2)
                    for m in (ident, ident_b):
                        pool.affine_select(out=m[:], in_=m[:], compare_op=ALU.not_equal, fill=1.0, base=0,
                                           pattern=[[-1, P]], channel_multiplier=1).then_inc(ident_ready, 1)
                    pool.wait_ge(ident_ready, 2)

                @block.vector
                def _(dve):
                    for b in range(B):
                        dve.wait_ge(x_loaded[b], 16)
                        with dve.Fori(b * TB, (b + 1) * TB) as t:
                            dve.bn_stats(stats[:, bass.ds(t, 1), :], x_all[:, bass.ds(t, 1), :]).then_inc(stats_ready, 1)
                    dve.wait_ge(stats_ready, T)

        def ffn(name, last):
            ln_scalars(name + "_ln")
            with ExitStack() as on:
                xn = sb(f"{name}_xn", [P, 2, GT, C], F32, on)
                xnt = sb(f"{name}_xnt", [P, 2, CC, 1 + W], F32, on)
                diff = sb(f"{name}_diff", [P, CC, W], F32, on)
                xr = sb(f"{name}_xr", [P, 2, CC, W], F32, on)
                xk = sb(f"{name}_xk", [P, 2, CC, W], F32, on)
                relu = sb(f"{name}_relu", [P, CC, W], F32, on)
                kact = sb(f"{name}_kact", [P, CC, W], F32, on)
                gate = sb(f"{name}_gate", [P, 2, 2 * C], F32, on)
                prod = sb(f"{name}_prod", [P, 2, 2, C], F32, on)
                ps_t = [ps(f"{name}_ps_t{c}", [P, W], F32, on) for c in range(CC)]
                ps_k = [ps(f"{name}_ps_k{c}", [P, W], F32, on) for c in range(CC)]
                ps_r = [ps(f"{name}_ps_r{c}", [P, 2 * C], F32, on) for c in range(2)]
                ps_o = [ps(f"{name}_ps_o{c}", [P, 2 * C], F32, on) for c in range(2)]
                xn_ready = sem(f"{name}_xn_ready", on)
                t_ready = sem(f"{name}_t_ready", on)
                xnt_ready = sem(f"{name}_xnt_ready", on)
                diff_ready = sem(f"{name}_diff_ready", on)
                mix_ready = sem(f"{name}_mix_ready", on)
                k_ready = sem(f"{name}_k_ready", on)
                relu_ready = sem(f"{name}_relu_ready", on)
                kact_ready = sem(f"{name}_kact_ready", on)
                r_ready = sem(f"{name}_r_ready", on)
                gate_ready = sem(f"{name}_gate_ready", on)
                o_ready = sem(f"{name}_o_ready", on)
                prod_ready = sem(f"{name}_prod_ready", on)
                x_ready = sem(f"{name}_x_ready", on)
                counted = sem(f"{name}_counted", on)
                stored = sem(f"{name}_stored", on)

                with nc.Block() as block:
                    @block.tensor
                    def _(pe):
                        def turn(g, par):
                            after(pe, xn_ready, g + 1)
                            after(pe, xnt_ready, 3 * g)
                            for c in range(CC):
                                for t in range(GT):
                                    ins = pe.transpose(ps_t[c][:, t * P:(t + 1) * P],
                                                       xn[:, par, t, c * P:(c + 1) * P], ident[:])
                                ins.then_inc(t_ready, 1)

                        def batch(i):
                            for j in range(GB):
                                g, par = i * GB + j, j % 2
                                after(pe, mix_ready, 4 * (g + 1))
                                after(pe, relu_ready, CC * g)
                                for m in range(CC):
                                    for c in range(CC):
                                        ins = pe.matmul(ps_k[m][:], w_k[:, c, m * P:(m + 1) * P],
                                                        xk[:, par, c, :], start=(c == 0), stop=(c == CC - 1))
                                    ins.then_inc(k_ready, 1)
                                if not (isinstance(i, int) and i == B - 1 and j == GB - 1):
                                    turn(g + 1, 1 - par)
                                for pair in range(2):
                                    after(pe, gate_ready, 2 * g + pair - 1)
                                    for t in range(2 * pair, 2 * pair + 2):
                                        for c in range(CC):
                                            ins = pe.matmul(ps_r[pair][:, (t % 2) * C:(t % 2 + 1) * C],
                                                            xr[:, par, c, t * P:(t + 1) * P], w_r[:, c, :],
                                                            start=(c == 0), stop=(c == CC - 1))
                                    ins.then_inc(r_ready, 1)
                                after(pe, kact_ready, g + 1)
                                for pair in range(2):
                                    after(pe, prod_ready, 2 * g + pair - 1)
                                    for t in range(2 * pair, 2 * pair + 2):
                                        for c in range(CC):
                                            ins = pe.matmul(ps_o[pair][:, (t % 2) * C:(t % 2 + 1) * C],
                                                            kact[:, c, t * P:(t + 1) * P], w_v[:, c, :],
                                                            start=(c == 0), stop=(c == CC - 1))
                                    ins.then_inc(o_ready, 1)

                        turn(0, 0)
                        looped(pe, B, batch)

                    @block.scalar
                    def _(act):
                        def normalize(g, par):
                            after(act, t_ready, CC * (g - 1))
                            for t in range(GT):
                                tile = g * GT + t
                                ins = act.activation(xn[:, par, t:t + 1, :], x_all[:, bass.ds(tile, 1), :], ACT.Identity,
                                                     bias=shift[:, bass.ds(tile, 1)], scale=rstd[:, bass.ds(tile, 1)])
                            ins.then_inc(xn_ready, 1)

                        def batch(i):
                            for j in range(GB):
                                g = i * GB + j
                                if not (isinstance(i, int) and i == B - 1 and j >= GB - 1):
                                    normalize(g + 1, (j + 1) % 2)
                                for m in range(CC):
                                    after(act, k_ready, CC * g + m + 1)
                                    after(act, kact_ready, g)
                                    act.activation(relu[:, m, :], ps_k[m][:], ACT.Relu).then_inc(relu_ready, 1)
                                for pair in range(2):
                                    after(act, r_ready, 2 * g + pair + 1)
                                    after(act, prod_ready, 2 * g + pair - 1)
                                    act.activation(gate[:, pair, :], ps_r[pair][:], ACT.Tanh,
                                                   scale=0.5).then_inc(gate_ready, 1)

                        normalize(0, 0)
                        looped(act, B, batch)

                    @block.gpsimd
                    def _(pool):
                        def batch(i):
                            for j in range(GB):
                                g = i * GB + j
                                after(pool, relu_ready, CC * (g + 1))
                                after(pool, o_ready, 2 * g)
                                pool.tensor_tensor(kact[:], relu[:], relu[:], ALU.mult).then_inc(kact_ready, 1)

                        looped(pool, B, batch)

                    @block.vector
                    def _(dve):
                        def mix(g, par, first):
                            after(dve, r_ready, 2 * (g - 1))
                            if first:
                                dve.memset(xnt[:, par, :, 0:1], 0.0).then_inc(xnt_ready, 1)
                            else:
                                dve.tensor_copy(xnt[:, par, :, 0:1], xnt[:, 1 - par, :, W:W + 1]).then_inc(xnt_ready, 1)
                            for c in range(CC):
                                after(dve, t_ready, CC * g + c + 1)
                                dve.tensor_copy(xnt[:, par, c, 1:1 + W], ps_t[c][:]).then_inc(xnt_ready, 1)
                            after(dve, xnt_ready, 3 * (g + 1))
                            after(dve, mix_ready, 4 * g)
                            dve.tensor_tensor(diff[:], xnt[:, par, :, 1:1 + W], xnt[:, par, :, 0:W],
                                              ALU.subtract).then_inc(diff_ready, 1)
                            after(dve, diff_ready, g + 1)
                            for dst, mu in ((xk, mu_kt), (xr, mu_rt)):
                                for c in range(CC):
                                    dve.scalar_tensor_tensor(out=dst[:, par, c, :], in0=diff[:, c, :],
                                                             scalar=mu[:, c:c + 1], in1=xnt[:, par, c, 0:W],
                                                             op0=ALU.mult, op1=ALU.add).then_inc(mix_ready, 1)

                        def batch(i):
                            for j in range(GB):
                                g = i * GB + j
                                if not (isinstance(i, int) and i == B - 1 and j == GB - 1):
                                    mix(g + 1, (j + 1) % 2, j == GB - 1)
                                for pair in range(2):
                                    n = 2 * g + pair
                                    tile = n * 2
                                    after(dve, gate_ready, n + 1)
                                    after(dve, o_ready, n + 1)
                                    after(dve, x_ready, n - 1)
                                    dve.scalar_tensor_tensor(
                                        out=prod[:, pair, :, :], in0=gate[:, pair, :].rearrange("p (t c) -> p t c", t=2),
                                        scalar=1.0, in1=ps_o[pair][:].rearrange("p (t c) -> p t c", t=2),
                                        op0=ALU.add, op1=ALU.mult).then_inc(prod_ready, 1)
                                    after(dve, prod_ready, n + 1)
                                    here = x_all[:, bass.ds(tile, 2), :]
                                    dve.scalar_tensor_tensor(out=here, in0=prod[:, pair, :, :], scalar=0.25, in1=here,
                                                             op0=ALU.mult, op1=ALU.add).then_inc(x_ready, 1)
                                    if not last:
                                        after(dve, x_ready, n + 1)
                                        for t in range(2):
                                            dve.bn_stats(stats[:, bass.ds(tile + t, 1), :],
                                                         x_all[:, bass.ds(tile + t, 1), :]).then_inc(counted, 1)

                        mix(0, 0, True)
                        looped(dve, B, batch)
                        dve.wait_ge(x_ready, 2 * G)
                        if not last:
                            dve.wait_ge(counted, T)

                    if last:
                        @block.sync
                        def _(sp):
                            with sp.Fori(0, G) as g:
                                tile = snap(sp, g * GT)
                                sp.wait_ge(x_ready, 2 * g + 2)
                                sp.dma_start(out_tiles[:, bass.ds(tile, GT), :],
                                             x_all[:, bass.ds(tile, GT), :]).then_inc(stored, 16)
                            sp.wait_ge(stored, 16 * G)

        ffn("ffn1", False)

        v_all = sb("v_all", [P, T, C], F32)

        ln_scalars("attn_ln")
        with ExitStack() as on:
            cos_t = sb("cos_t", [P, N], F32, on)
            sin_t = sb("sin_t", [P, N], F32, on)
            xn = sb("a_xn", [P, 2, GT, C], F32, on)
            xnt = sb("a_xnt", [P, 2, CC, W], F32, on)
            qk = sb("qk", [P, 2, CC, W], F32, on)
            swapped = sb("swapped", [P, 2, CC, W], F32, on)
            part = sb("part", [P, 2, PARTS, CC, W], BF16, on)
            ps_t = [ps(f"a_ps_t{c}", [P, W], F32, on) for c in range(CC)]
            ps_q = [ps(f"a_ps_q{c}", [P, W], F32, on) for c in range(2 * CC)]
            ps_v = [ps(f"a_ps_v{c}", [P, 2 * C], F32, on) for c in range(2)]
            tab_loaded = sem("tab_loaded", on)
            xn_ready = sem("a_xn_ready", on)
            t_ready = sem("a_t_ready", on)
            xnt_ready = sem("a_xnt_ready", on)
            q_ready = sem("q_ready", on)
            qk_ready = sem("qk_ready", on)
            swap_in = [sem(f"swap_in{a}", on) for a in range(2)]
            sin_ready = sem("sin_ready", on)
            cos_ready = sem("cos_ready", on)
            rope_ready = sem("rope_ready", on)
            high_ready = sem("high_ready", on)
            rest_ready = sem("rest_ready", on)
            mid_ready = sem("mid_ready", on)
            low_ready = sem("low_ready", on)
            sent = [sem(f"sent{a}", on) for a in range(2)]
            v_ready = sem("a_v_ready", on)
            v_kept = sem("v_kept", on)

            with nc.Block() as block:
                @block.sync
                def _(sp):
                    sp.dma_start(cos_t[:], cos).then_inc(tab_loaded, 16)
                    sp.dma_start(sin_t[:], sin).then_inc(tab_loaded, 16)

                    def swap(g, a):
                        made, used = snap(sp, CC * (2 * g + a + 1)), snap(sp, 2 * g + a - 1)
                        after(sp, qk_ready, made)
                        after(sp, rope_ready, used)
                        for odd in range(2):
                            sp.dma_start(swapped[odd::2, a, :, :], qk[1 - odd::2, a, :, :]).then_inc(swap_in[a], 16)

                    def send(g, a):
                        after(sp, low_ready, 2 * g + a + 1)
                        for s in range(PARTS):
                            sp.dma_start(split_dram[a, s, :, bass.ds(g * W, W)].rearrange("(c p) n -> p c n", p=P),
                                         part[:, a, s, :, :]).then_inc(sent[a], 16)

                    def batch(i):
                        for j in range(GB):
                            g = i * GB + j
                            swap(g, 0)
                            swap(g, 1)
                            send(g, 0)
                            send(g, 1)

                    looped(sp, B, batch)
                    for a in range(2):
                        sp.wait_ge(sent[a], 16 * PARTS * G)

                @block.tensor
                def _(pe):
                    def turn(g, par):
                        after(pe, xn_ready, g + 1)
                        after(pe, xnt_ready, CC * g)
                        for c in range(CC):
                            for t in range(GT):
                                ins = pe.transpose(ps_t[c][:, t * P:(t + 1) * P],
                                                   xn[:, par, t, c * P:(c + 1) * P], ident[:])
                            ins.then_inc(t_ready, 1)

                    def batch(i):
                        for j in range(GB):
                            g, par = i * GB + j, j % 2
                            after(pe, xnt_ready, CC * (g + 1))
                            for m in range(2 * CC):
                                after(pe, qk_ready, 2 * CC * (g - 1) + m + 1)
                                for c in range(CC):
                                    ins = pe.matmul(ps_q[m][:], w_qkv[:, c, m * P:(m + 1) * P], xnt[:, par, c, :],
                                                    start=(c == 0), stop=(c == CC - 1))
                                ins.then_inc(q_ready, 1)
                                if m == CC - 1 and not (isinstance(i, int) and i == B - 1 and j == GB - 1):
                                    turn(g + 1, 1 - par)
                            for pair in range(2):
                                after(pe, v_kept, 2 * g + pair - 1)
                                for t in range(2 * pair, 2 * pair + 2):
                                    for c in range(CC):
                                        ins = pe.matmul(ps_v[pair][:, (t % 2) * C:(t % 2 + 1) * C],
                                                        xnt[:, par, c, t * P:(t + 1) * P], w_qkv[:, c, 2 * C:3 * C],
                                                        start=(c == 0), stop=(c == CC - 1))
                                ins.then_inc(v_ready, 1)

                    turn(0, 0)
                    looped(pe, B, batch)

                @block.scalar
                def _(act):
                    def normalize(g, par):
                        after(act, t_ready, CC * (g - 1))
                        for t in range(GT):
                            tile = g * GT + t
                            ins = act.activation(xn[:, par, t:t + 1, :], x_all[:, bass.ds(tile, 1), :], ACT.Identity,
                                                 bias=shift[:, bass.ds(tile, 1)], scale=rstd[:, bass.ds(tile, 1)])
                        ins.then_inc(xn_ready, 1)

                    def batch(i):
                        for j in range(GB):
                            g = i * GB + j
                            if not (isinstance(i, int) and i == B - 1 and j >= GB - 1):
                                normalize(g + 1, (j + 1) % 2)
                            for a in range(2):
                                after(act, low_ready, 2 * (g - 1) + a + 1)
                                for c in range(CC):
                                    m = a * CC + c
                                    after(act, q_ready, 2 * CC * g + m + 1)
                                    act.activation(qk[:, a, c, :], ps_q[m][:], ACT.Identity,
                                                   bias=b_qk[:, m:m + 1]).then_inc(qk_ready, 1)
                            for a in range(2):
                                after(act, rope_ready, 2 * g + a + 1)
                                after(act, sent[a], 16 * PARTS * g)
                                act.activation(part[:, a, 0, :, :], qk[:, a, :, :], ACT.Copy).then_inc(high_ready, 1)
                                after(act, rest_ready, 2 * g + a + 1)
                                act.activation(part[:, a, 1, :, :], qk[:, a, :, :], ACT.Copy).then_inc(mid_ready, 1)

                    normalize(0, 0)
                    looped(act, B, batch)

                @block.gpsimd
                def _(pool):
                    pool.wait_ge(tab_loaded, 32)

                    def batch(i):
                        for j in range(GB):
                            g = i * GB + j
                            for a in range(2):
                                after(pool, swap_in[a], 32 * (g + 1))
                                for c in range(CC):
                                    ins = pool.tensor_tensor(swapped[:, a, c, :], swapped[:, a, c, :],
                                                             sin_t[:, j * W:(j + 1) * W], ALU.mult)
                                    ins.then_inc(sin_ready, 1)

                    looped(pool, B, batch)

                @block.vector
                def _(dve):
                    dve.wait_ge(tab_loaded, 32)

                    def take_turned(g, par):
                        after(dve, v_ready, 2 * (g - 1))
                        for c in range(CC):
                            after(dve, t_ready, CC * g + c + 1)
                            dve.tensor_copy(xnt[:, par, c, :], ps_t[c][:]).then_inc(xnt_ready, 1)

                    def batch(i):
                        for j in range(GB):
                            g = i * GB + j
                            if not (isinstance(i, int) and i == B - 1 and j == GB - 1):
                                take_turned(g + 1, (j + 1) % 2)
                            for a in range(2):
                                after(dve, swap_in[a], 32 * (g + 1))
                                for c in range(CC):
                                    dve.tensor_tensor(qk[:, a, c, :], qk[:, a, c, :], cos_t[:, j * W:(j + 1) * W],
                                                      ALU.mult).then_inc(cos_ready, 1)
                                after(dve, cos_ready, CC * (2 * g + a + 1))
                                after(dve, sin_ready, CC * (2 * g + a + 1))
                                dve.tensor_tensor(qk[:, a, :, :], qk[:, a, :, :], swapped[:, a, :, :],
                                                  ALU.add).then_inc(rope_ready, 1)
                                pair = a
                                after(dve, v_ready, 2 * g + pair + 1)
                                for t in range(2):
                                    tile = g * GT + 2 * pair + t
                                    ins = dve.tensor_tensor(v_all[:, bass.ds(tile, 1), :].rearrange("p t c -> p (t c)"),
                                                            ps_v[pair][:, t * C:(t + 1) * C], b_v[:], ALU.add)
                                ins.then_inc(v_kept, 1)
                            for a in range(2):
                                after(dve, high_ready, 2 * g + a + 1)
                                dve.tensor_tensor(qk[:, a, :, :], qk[:, a, :, :], part[:, a, 0, :, :],
                                                  ALU.subtract).then_inc(rest_ready, 1)
                                after(dve, mid_ready, 2 * g + a + 1)
                                dve.tensor_tensor(part[:, a, 2, :, :], qk[:, a, :, :], part[:, a, 1, :, :],
                                                  ALU.subtract).then_inc(low_ready, 1)

                    take_turned(0, 0)
                    looped(dve, B, batch)
                    dve.wait_ge(v_kept, 2 * G)

        with ExitStack() as on:
            LEAD = TB + TB // 4
            SLOTS = HEADS * TB
            q_a = sb("q_a", [R, 2, N], BF16, on)
            k_a = sb("k_a", [R, 2, N], BF16, on)
            q_b = sb("q_b", [R + PARTS, 2, N], BF16, on)
            k_b = sb("k_b", [R + PARTS, 2, N], BF16, on)
            probs = sb("probs", [P, 2, N], F32, on)
            VW = 2 * D
            v_h = sb("v_h", [P, 2, TB, VW], F32, on)
            half_max = sb("half_max", [P, 2, TB, 2], F32, on)
            neg_max = sb("neg_max", [P, TB], F32, on)
            max_part = sb("max_part", [P, PARTS, TB], BF16, on)
            max_rows = sb("max_rows", [PARTS * TB, P], BF16, on)
            o_t = sb("o_t", [P, W], F32, on)
            recip = sb("recip", [P, NJ, NJ], F32, on)
            ps_e = [ps(f"ps_e{n}", [P, W], F32, on) for n in range(2)]
            ps_m = [ps(f"ps_m{n}", [P, 2, W], F32, on) for n in range(2)]
            ps_o = ps("ps_o", [P, W], F32, on)
            ps_x = ps("ps_x", [P, W], F32, on)

            def head_slice(h):
                return v_all[:, bass.ds(h // H * TB, TB), bass.ds(h % H * D, D)]

            ones_ready = sem("ones_ready", on)
            a_loaded = sem("a_loaded", on)
            b_loaded = sem("b_loaded", on)
            m_loaded = sem("m_loaded", on)
            v_copied = sem("v_copied", on)
            e_ready = sem("e_ready", on)
            exp_done = sem("exp_done", on)
            s_ready = sem("s_ready", on)
            max_done = sem("max_done", on)
            split = sem("split", on)
            rows_ready = sem("rows_ready", on)
            rows_taken = sem("rows_taken", on)
            pv_done = sem("pv_done", on)
            o_taken = sem("o_taken", on)
            o_turned = sem("o_turned", on)
            recip_done = sem("recip_done", on)
            o_kept = sem("o_kept", on)

            with nc.Block() as block:
                @block.sync
                def _(sp):
                    def load_a(h, par):
                        row, col = h % H * D, h // H * N
                        row, col = snap(sp, row), snap(sp, col)
                        made, copied = snap(sp, 2 * TB * (h - 1)), snap(sp, 32 * (h - 1))
                        after(sp, s_ready, made)
                        after(sp, b_loaded, copied)
                        for n, (a, b) in enumerate(PAIRS):
                            for side, s, dst in ((0, a, q_a), (1, b, k_a)):
                                src = split_dram[side, s, bass.ds(row, D), bass.ds(col, N)]
                                sp.dma_start(dst[n * D:(n + 1) * D, par, :], src).then_inc(a_loaded, 16)

                    def copy_b(h, par):
                        loaded, copied = snap(sp, 32 * len(PAIRS) * (h + 1)), snap(sp, 32 * h)
                        used = snap(sp, NJ * TB * (h - 1))
                        after(sp, a_loaded, loaded)
                        after(sp, b_loaded, copied)
                        after(sp, e_ready, used)
                        sp.dma_start(q_b[0:R, par, :], q_a[:, par, :]).then_inc(b_loaded, 16)
                        sp.dma_start(k_b[0:R, par, :], k_a[:, par, :]).then_inc(b_loaded, 16)

                    def load_max(h, par):
                        after(sp, rows_taken, h + 1)
                        sp.dma_start(q_b[R:R + PARTS, par, :], max_rows[:]).then_inc(m_loaded, 16)

                    def two_heads(i):
                        for e in range(2):
                            h = 2 * i + e + 1
                            if isinstance(i, int) and h >= HEADS:
                                continue
                            copy_b(h, (e + 1) % 2)
                            if not (isinstance(i, int) and h + 1 >= HEADS):
                                load_a(h + 1, e)
                            load_max(h, (e + 1) % 2)

                    load_a(0, 0)
                    copy_b(0, 0)
                    load_a(1, 1)
                    load_max(0, 0)
                    looped(sp, HEADS // 2, two_heads)

                @block.gpsimd
                def _(pool):
                    pool.memset(v_h[:], 1.0).then_inc(ones_ready, 1)
                    pool.wait_ge(ones_ready, 1)
                    pool.memset(k_b[R:R + PARTS, :, :], 1.0).then_inc(ones_ready, 1)
                    pool.wait_ge(ones_ready, 2)

                    def two_heads(i):
                        for e in range(2):
                            h = 2 * i + e
                            after(pool, pv_done, TB * (h - 1))
                            pool.tensor_copy(v_h[:, e, :, 0:D], head_slice(h)).then_inc(v_copied, 1)

                    looped(pool, HEADS // 2, two_heads)

                @block.tensor
                def _(pe):
                    def score_max(m, j, par, t):
                        if j % 2 == 0:
                            after(pe, max_done, 2 * m + j // 2 - 1)
                        ins = pe.matmul(ps_m[j // 2][:, j % 2, :], q_a[:, par, t * P:(t + 1) * P],
                                        k_a[:, par, j * W:(j + 1) * W], start=True, stop=True)
                        if j % 2 == 1:
                            ins.then_inc(s_ready, 1)

                    def turn_max(h):
                        after(pe, split, 5 * (h + 1))
                        after(pe, o_kept, h - 1)
                        pe.matmul(ps_x[0:PARTS * TB, 0:P], max_part[:].rearrange("p s t -> p (s t)"), ident_b[:],
                                  start=True, stop=True).then_inc(rows_ready, 1)

                    def turn_out(h):
                        after(pe, o_taken, h + 1)
                        after(pe, rows_taken, h + 2)
                        for s in range(W // P):
                            ins = pe.transpose(ps_x[:, s * P:(s + 1) * P], o_t[:, s * P:(s + 1) * P], ident[:])
                        ins.then_inc(o_turned, 1)

                    def pv(k, par, kt):
                        after(pe, exp_done, NJ * (k + 1))
                        for j in range(NJ):
                            ins = pe.matmul(ps_o[VW * j:VW * (j + 1), :], v_h[:, par, kt, :],
                                            probs[:, kt % 2, j * W:(j + 1) * W], start=(kt == 0), stop=(kt == TB - 1))
                        ins.then_inc(pv_done, 1)

                    def two_heads(i):
                        for s in range(2 * TB):
                            e, kt = s // TB, s % TB
                            k = i * (2 * TB) + s
                            h = 2 * i + e
                            m = k + LEAD
                            ahead = (s + LEAD) // TB % 2
                            has_max = not (isinstance(i, int) and m >= SLOTS)
                            if kt == 0:
                                after(pe, b_loaded, 32 * (h + 1))
                                after(pe, m_loaded, 16 * (h + 1))
                            if has_max and (s + LEAD) % TB == 0:
                                after(pe, a_loaded, 32 * len(PAIRS) * (2 * i + (s + LEAD) // TB + 1))
                            for j in range(NJ):
                                after(pe, exp_done, NJ * k + j - 1)
                                pe.matmul(ps_e[j % 2][:], k_b[:, e, kt * P:(kt + 1) * P],
                                          q_b[:, e, j * W:(j + 1) * W], start=True, stop=True).then_inc(e_ready, 1)
                                if has_max:
                                    score_max(m, j, ahead, (s + LEAD) % TB)
                            if kt == 3 and not (isinstance(i, int) and h == 0):
                                turn_out(h - 1)
                            if kt == 13 and not (isinstance(i, int) and h + 1 >= HEADS):
                                turn_max(h + 1)
                            if kt == 0:
                                if not (isinstance(i, int) and h == 0):
                                    pv(k - 1, 1 - e, TB - 1)
                            else:
                                if kt == 1:
                                    after(pe, v_copied, h + 1)
                                    after(pe, o_taken, h)
                                pv(k - 1, e, kt - 1)

                    pe.wait_ge(ones_ready, 2)
                    for m in range(LEAD):
                        if m % TB == 0:
                            after(pe, a_loaded, 32 * len(PAIRS) * (m // TB + 1))
                        for j in range(NJ):
                            score_max(m, j, m // TB, m % TB)
                    turn_max(0)
                    looped(pe, HEADS // 2, two_heads)
                    pv(SLOTS - 1, 1, TB - 1)
                    after(pe, o_taken, HEADS)
                    after(pe, o_kept, HEADS - 1)
                    for s in range(W // P):
                        ins = pe.transpose(ps_x[:, s * P:(s + 1) * P], o_t[:, s * P:(s + 1) * P], ident[:])
                    ins.then_inc(o_turned, 1)

                @block.scalar
                def _(act):
                    def take_rows(h):
                        after(act, rows_ready, h + 1)
                        after(act, m_loaded, 16 * h)
                        act.activation(max_rows[:], ps_x[0:PARTS * TB, 0:P], ACT.Copy).then_inc(rows_taken, 1)

                    def take_out(h):
                        after(act, pv_done, TB * (h + 1))
                        after(act, o_turned, h)
                        act.activation(o_t[:], ps_o[:], ACT.Copy).then_inc(o_taken, 1)

                    def two_heads(i):
                        for s in range(2 * TB):
                            e, kt = s // TB, s % TB
                            k = i * (2 * TB) + s
                            h = 2 * i + e
                            for j in range(NJ):
                                after(act, e_ready, NJ * k + j + 1)
                                if j == 0:
                                    after(act, pv_done, k - 1)
                                act.activation(probs[:, kt % 2, j * W:(j + 1) * W], ps_e[j % 2][:], ACT.Exp,
                                               scale=scale).then_inc(exp_done, 1)
                            if kt == 0 and not (isinstance(i, int) and h == 0):
                                take_out(h - 1)
                            if kt == 13 and not (isinstance(i, int) and h + 1 >= HEADS):
                                take_rows(h + 1)

                    take_rows(0)
                    looped(act, HEADS // 2, two_heads)
                    take_out(HEADS - 1)

                @block.vector
                def _(dve):
                    def slot_max(m, par, t):
                        for half in range(2):
                            after(dve, s_ready, 2 * m + half + 1)
                            dve.tensor_reduce(half_max[:, par, t, half:half + 1], ps_m[half][:], AX.XY,
                                              ALU.max).then_inc(max_done, 1)

                    def split_max(h, par):
                        after(dve, max_done, 2 * TB * (h + 1))
                        dve.tensor_reduce(neg_max[:], half_max[:, par, :, :], AX.X, ALU.max,
                                          negate=True).then_inc(split, 1)
                        after(dve, rows_ready, h)
                        for s in range(PARTS - 1):
                            after(dve, split, 5 * h + 2 * s + 1)
                            dve.tensor_copy(max_part[:, s, :], neg_max[:]).then_inc(split, 1)
                            after(dve, split, 5 * h + 2 * s + 2)
                            rest = neg_max[:] if s < PARTS - 2 else max_part[:, PARTS - 1, :]
                            dve.tensor_tensor(rest, neg_max[:], max_part[:, s, :], ALU.subtract).then_inc(split, 1)

                    def keep_out(h):
                        after(dve, o_turned, h + 1)
                        turned = ps_x[:].rearrange("p (s j d) -> p s j d", j=NJ, d=VW)
                        after(dve, o_kept, h)
                        dve.reciprocal(recip[:], turned[:, :, :, D]).then_inc(recip_done, 1)
                        after(dve, recip_done, h + 1)
                        dst = head_slice(h).rearrange("p (j s) d -> p s j d", j=NJ)
                        dve.tensor_tensor(dst, turned[:, :, :, 0:D],
                                          recip[:].rearrange("p s (j o) -> p s j o", o=1).broadcast_to([P, NJ, NJ, D]),
                                          ALU.mult).then_inc(o_kept, 1)

                    def two_heads(i):
                        for s in range(2 * TB):
                            e, kt = s // TB, s % TB
                            k = i * (2 * TB) + s
                            h = 2 * i + e
                            if not (isinstance(i, int) and k + LEAD >= SLOTS):
                                slot_max(k + LEAD, (s + LEAD) // TB % 2, (s + LEAD) % TB)
                            if kt == 11 and not (isinstance(i, int) and h + 1 >= HEADS):
                                split_max(h + 1, 1 - e)
                            if kt == 4 and not (isinstance(i, int) and h == 0):
                                keep_out(h - 1)

                    for m in range(LEAD):
                        slot_max(m, m // TB, m % TB)
                        if m == TB - 1:
                            split_max(0, 0)
                    looped(dve, HEADS // 2, two_heads)
                    keep_out(HEADS - 1)
                    dve.wait_ge(o_kept, HEADS)

        with ExitStack() as on:
            attn = sb("attn", [P, 2, GT, C], F32, on)
            attn_t = sb("attn_t", [P, 2, CC, W], F32, on)
            ps_t = [ps(f"p_ps_t{c}", [P, W], F32, on) for c in range(2 * CC)]
            ps_y = [ps(f"p_ps_y{c}", [P, 2, C], F32, on) for c in range(2)]
            attn_ready = sem("attn_ready", on)
            t_ready = sem("p_t_ready", on)
            attn_t_ready = sem("attn_t_ready", on)
            y_ready = sem("y_ready", on)
            sum_ready = sem("sum_ready", on)
            x_ready = sem("p_x_ready", on)
            counted = sem("p_counted", on)

            with nc.Block() as block:
                @block.gpsimd
                def _(pool):
                    def batch(i):
                        for j in range(GB):
                            g = i * GB + j
                            after(pool, t_ready, CC * (g - 1))
                            pool.tensor_copy(attn[:, j % 2, :, :], v_all[:, bass.ds(g * GT, GT), :]).then_inc(attn_ready, 1)

                    looped(pool, B, batch)

                @block.tensor
                def _(pe):
                    def turn(g, par):
                        after(pe, attn_ready, g + 1)
                        after(pe, attn_t_ready, CC * (g - 1))
                        for c in range(CC):
                            for t in range(GT):
                                ins = pe.transpose(ps_t[par * CC + c][:, t * P:(t + 1) * P],
                                                   attn[:, par, t, c * P:(c + 1) * P], ident[:])
                            ins.then_inc(t_ready, 1)

                    def batch(i):
                        for j in range(GB):
                            g, par = i * GB + j, j % 2
                            if not (isinstance(i, int) and i == B - 1 and j == GB - 1):
                                turn(g + 1, 1 - par)
                            after(pe, attn_t_ready, CC * (g + 1))
                            for pair in range(2):
                                after(pe, sum_ready, 2 * g + pair - 1)
                                for t in range(2 * pair, 2 * pair + 2):
                                    for c in range(CC):
                                        ins = pe.matmul(ps_y[pair][:, t % 2, :], attn_t[:, par, c, t * P:(t + 1) * P],
                                                        w_proj[:, c, :], start=(c == 0), stop=(c == CC - 1))
                                ins.then_inc(y_ready, 1)

                    turn(0, 0)
                    looped(pe, B, batch)

                @block.scalar
                def _(act):
                    def batch(i):
                        for j in range(GB):
                            g, par = i * GB + j, j % 2
                            after(act, y_ready, 2 * (g - 1))
                            for c in range(CC):
                                after(act, t_ready, CC * g + c + 1)
                                act.activation(attn_t[:, par, c, :], ps_t[par * CC + c][:],
                                               ACT.Copy).then_inc(attn_t_ready, 1)

                    looped(act, B, batch)

                @block.vector
                def _(dve):
                    def batch(i):
                        for n0 in range(2 * GB):
                            n, pair = i * 2 * GB + n0, n0 % 2
                            here = x_all[:, bass.ds(2 * n, 2), :]
                            after(dve, y_ready, n + 1)
                            dve.tensor_tensor(here, here, ps_y[pair][:], ALU.add).then_inc(sum_ready, 1)
                            after(dve, sum_ready, n + 1)
                            dve.tensor_tensor(here, here, b_proj[:].rearrange("p (o c) -> p o c", o=1)
                                              .broadcast_to([P, 2, C]), ALU.add).then_inc(x_ready, 1)
                            after(dve, x_ready, n + 1)
                            for t in range(2):
                                dve.bn_stats(stats[:, bass.ds(2 * n + t, 1), :],
                                             x_all[:, bass.ds(2 * n + t, 1), :]).then_inc(counted, 1)

                    looped(dve, B, batch)
                    dve.wait_ge(counted, T)

        ffn("ffn2", True)


def kernel(L0_attn_x, L0_attn_qkv_w, L0_attn_qkv_b, L0_attn_proj_w, L0_attn_proj_b, L0_ffn_W_r, L0_ffn_W_k,
           L0_ffn_W_v, L0_ffn_mu_r, L0_ffn_mu_k):
    import numpy as np
    import concourse.bacc as bacc
    from concourse.bass_utils import run_bass_kernel_spmd

    B, N, C = L0_attn_x.shape
    D = C // 16
    inv = np.float32(1.0) / np.float32(10000.0) ** (np.arange(0, D, 2, dtype=np.float32) / np.float32(D))
    angle = np.arange(N, dtype=np.float32)[None, :] * inv.astype(np.float32)[:, None]
    rows = (np.arange(P) % D) // 2
    sign = np.where(np.arange(P) % 2 == 0, -1.0, 1.0).astype(np.float32)[:, None]

    def columns(v):
        return np.asarray(v).reshape(-1, P).T

    arrays = {
        "x": L0_attn_x, "wr_t": L0_ffn_W_r.T, "wk_t": L0_ffn_W_k.T, "wv_t": L0_ffn_W_v.T,
        "mu_r": columns(L0_ffn_mu_r), "mu_k": columns(L0_ffn_mu_k),
        "qkv_t": L0_attn_qkv_w.T, "qk_b": columns(L0_attn_qkv_b[:2 * C]), "qkv_b": L0_attn_qkv_b,
        "proj_t": L0_attn_proj_w.T, "proj_b": L0_attn_proj_b,
        "cos": np.cos(angle)[rows], "sin": np.sin(angle)[rows] * sign,
    }
    arrays = {f"in_{k}": np.ascontiguousarray(np.asarray(v)) for k, v in arrays.items()}
    nc = bacc.Bacc("TRN2", target_bir_lowering=False, num_devices=1)
    args = [nc.dram_tensor(k, v.shape, F32, kind="ExternalInput").ap() for k, v in arrays.items()]
    out = nc.dram_tensor("out_0", (B, N, C), F32, kind="ExternalOutput").ap()
    macaron(nc, *args, out)
    r = run_bass_kernel_spmd(nc, [arrays], core_ids=[0])
    return r.results[0]["out_0"]
```

```python
from contextlib import ExitStack

import concourse.bass as bass
from concourse import mybir

F32 = mybir.dt.float32
BF16 = mybir.dt.bfloat16
I32 = mybir.dt.int32
ALU = mybir.AluOpType
ACT = mybir.ActivationFunctionType
AX = mybir.AxisListType

P = 128
EPS = 1e-5
PARTS = 3
PAIRS = [(0, 0), (0, 1), (0, 2), (1, 0), (1, 1), (2, 0)]


def some(count):
    return not isinstance(count, int) or count > 0


def snap(eng, value):
    return value if isinstance(value, int) else eng.snap(eng.to_reg(value))


def looped(eng, n, step):
    step(0)
    with eng.Fori(1, n - 1) as i:
        step(i)
    step(n - 1)


def macaron(nc, x, wr_t, wk_t, wv_t, mu_r, mu_k, qkv_t, qk_b, qkv_b, proj_t, proj_b, cos, sin, out):
    B, N, C = x.shape
    H, D = 16, C // 16
    T = B * N // P
    GT = 4
    W = GT * P
    G = T // GT
    GB = G // B
    CC = C // P
    TB = T // B
    HEADS = B * H
    R = len(PAIRS) * D
    NJ = N // W
    scale = float(D) ** -0.5

    x_tiles = x.rearrange("b (t p) c -> p (b t) c", p=P)
    out_tiles = out.rearrange("b (t p) c -> p (b t) c", p=P)
    split_dram = nc.dram_tensor("split_dram", (2, PARTS, C, B * N), BF16, kind="Internal").ap()

    ctx = ExitStack()
    with ctx:
        def sb(name, shape, dt, on=ctx):
            return on.enter_context(nc.sbuf_tensor(name, shape, dt))

        def ps(name, shape, dt, on):
            return on.enter_context(nc.psum_tensor(name, shape, dt))

        def sem(name, on):
            return on.enter_context(nc.semaphore(name))

        x_all = sb("x_all", [P, T, C], F32)
        ident = sb("ident", [P, P], F32)
        ident_b = sb("ident_b", [P, P], BF16)
        w_r = sb("w_r", [P, CC, C], F32)
        w_k = sb("w_k", [P, CC, C], F32)
        w_v = sb("w_v", [P, CC, C], F32)
        w_qkv = sb("w_qkv", [P, CC, 3 * C], F32)
        w_proj = sb("w_proj", [P, CC, C], F32)
        mu_rt = sb("mu_rt", [P, CC], F32)
        mu_kt = sb("mu_kt", [P, CC], F32)
        b_qk = sb("b_qk", [P, 2 * CC], F32)
        b_v = sb("b_v", [P, C], F32)
        b_proj = sb("b_proj", [P, C], F32)
        stats = sb("stats", [P, T, 6], F32)
        rstd = sb("rstd", [P, T], F32)
        shift = sb("shift", [P, T], F32)

        def ln_scalars(name):
            with ExitStack() as on:
                half = sb(f"{name}_half", [P, T], F32, on)
                mean = sb(f"{name}_mean", [P, T], F32, on)
                var = sb(f"{name}_var", [P, T], F32, on)
                root = sb(f"{name}_root", [P, T], F32, on)
                var_ready = sem(f"{name}_var_ready", on)
                root_ready = sem(f"{name}_root_ready", on)
                chain = sem(f"{name}_chain", on)
                with nc.Block() as block:
                    @block.vector
                    def _(dve):
                        done = [0]

                        def link(ins):
                            done[0] += 1
                            ins.then_inc(chain, 1)
                            dve.wait_ge(chain, done[0])

                        even, odd = stats[:, :, 1], stats[:, :, 4]
                        dve.tensor_tensor(half[:], even, odd, ALU.subtract).then_inc(chain, 1)
                        dve.tensor_tensor(mean[:], even, odd, ALU.add).then_inc(chain, 1)
                        dve.tensor_tensor(var[:], stats[:, :, 2], stats[:, :, 5], ALU.add).then_inc(chain, 1)
                        done[0] = 3
                        dve.wait_ge(chain, 3)
                        link(dve.scalar_tensor_tensor(out=half[:], in0=half[:], scalar=0.25, in1=half[:],
                                                      op0=ALU.mult, op1=ALU.mult))
                        link(dve.scalar_tensor_tensor(out=var[:], in0=var[:], scalar=1.0 / C, in1=half[:],
                                                      op0=ALU.mult, op1=ALU.add))
                        dve.tensor_scalar(var[:], var[:], EPS, None, ALU.add).then_inc(var_ready, 1)
                        dve.wait_ge(root_ready, 1)
                        link(dve.reciprocal(rstd[:], root[:]))
                        link(dve.tensor_tensor(half[:], rstd[:], rstd[:], ALU.mult))
                        link(dve.tensor_tensor(half[:], half[:], var[:], ALU.mult))
                        link(dve.tensor_scalar(half[:], half[:], -0.5, 1.5, ALU.mult, ALU.add))
                        link(dve.tensor_tensor(rstd[:], rstd[:], half[:], ALU.mult))
                        link(dve.scalar_tensor_tensor(out=shift[:], in0=mean[:], scalar=-0.5, in1=rstd[:],
                                                      op0=ALU.mult, op1=ALU.mult))

                    @block.scalar
                    def _(act):
                        act.wait_ge(var_ready, 1)
                        act.activation(root[:], var[:], ACT.Sqrt).then_inc(root_ready, 1)

        with ExitStack() as on:
            x_loaded = [sem(f"x_loaded{b}", on) for b in range(B)]
            w_loaded = sem("w_loaded", on)
            zeroed = sem("zeroed", on)
            ident_ready = sem("ident_ready", on)
            stats_ready = sem("stats_ready", on)
            n_w = 12
            with nc.Block() as block:
                @block.sync
                def _(sp):
                    for b in range(B):
                        sp.dma_start(x_all[:, b * TB:(b + 1) * TB, :],
                                     x_tiles[:, b * TB:(b + 1) * TB, :]).then_inc(x_loaded[b], 16)

                @block.scalar
                def _(act):
                    chunked = "(c p) n -> p c n"
                    for dst, src in ((w_r, wr_t), (w_k, wk_t), (w_v, wv_t), (w_qkv, qkv_t), (w_proj, proj_t)):
                        act.dma_start(dst[:], src.rearrange(chunked, p=P)).then_inc(w_loaded, 16)
                    act.dma_start(mu_rt[:], mu_r).then_inc(w_loaded, 16)
                    act.dma_start(mu_kt[:], mu_k).then_inc(w_loaded, 16)
                    act.dma_start(b_qk[:], qk_b).then_inc(w_loaded, 16)
                    act.dma_start(b_v[:], qkv_b[2 * C:3 * C].rearrange("(o n) -> o n", o=1)
                                  .broadcast_to([P, C])).then_inc(w_loaded, 16)
                    act.dma_start(b_proj[:], proj_b.rearrange("(o n) -> o n", o=1)
                                  .broadcast_to([P, C])).then_inc(w_loaded, 16)
                    act.wait_ge(w_loaded, 16 * 10)

                @block.gpsimd
                def _(pool):
                    pool.memset(ident[:], 0.0).then_inc(zeroed, 1)
                    pool.memset(ident_b[:], 0.0).then_inc(zeroed, 1)
                    pool.wait_ge(zeroed, 2)
                    for m in (ident, ident_b):
                        pool.affine_select(out=m[:], in_=m[:], compare_op=ALU.not_equal, fill=1.0, base=0,
                                           pattern=[[-1, P]], channel_multiplier=1).then_inc(ident_ready, 1)
                    pool.wait_ge(ident_ready, 2)

                @block.vector
                def _(dve):
                    for b in range(B):
                        dve.wait_ge(x_loaded[b], 16)
                        with dve.Fori(b * TB, (b + 1) * TB) as t:
                            dve.bn_stats(stats[:, bass.ds(t, 1), :], x_all[:, bass.ds(t, 1), :]).then_inc(stats_ready, 1)
                    dve.wait_ge(stats_ready, T)

        def ffn(name, last):
            ln_scalars(name + "_ln")
            with ExitStack() as on:
                xn = sb(f"{name}_xn", [P, 2, GT, C], F32, on)
                xnt = sb(f"{name}_xnt", [P, 2, CC, 1 + W], F32, on)
                diff = sb(f"{name}_diff", [P, CC, W], F32, on)
                xr = sb(f"{name}_xr", [P, 2, CC, W], F32, on)
                xk = sb(f"{name}_xk", [P, 2, CC, W], F32, on)
                relu = sb(f"{name}_relu", [P, CC, W], F32, on)
                kact = sb(f"{name}_kact", [P, CC, W], F32, on)
                gate = sb(f"{name}_gate", [P, 2, 2 * C], F32, on)
                prod = sb(f"{name}_prod", [P, 2, 2, C], F32, on)
                ps_t = [ps(f"{name}_ps_t{c}", [P, W], F32, on) for c in range(CC)]
                ps_k = [ps(f"{name}_ps_k{c}", [P, W], F32, on) for c in range(CC)]
                ps_r = [ps(f"{name}_ps_r{c}", [P, 2 * C], F32, on) for c in range(2)]
                ps_o = [ps(f"{name}_ps_o{c}", [P, 2 * C], F32, on) for c in range(2)]
                xn_ready = sem(f"{name}_xn_ready", on)
                t_ready = sem(f"{name}_t_ready", on)
                xnt_ready = sem(f"{name}_xnt_ready", on)
                diff_ready = sem(f"{name}_diff_ready", on)
                mix_ready = sem(f"{name}_mix_ready", on)
                k_ready = sem(f"{name}_k_ready", on)
                relu_ready = sem(f"{name}_relu_ready", on)
                kact_ready = sem(f"{name}_kact_ready", on)
                r_ready = sem(f"{name}_r_ready", on)
                gate_ready = sem(f"{name}_gate_ready", on)
                o_ready = sem(f"{name}_o_ready", on)
                prod_ready = sem(f"{name}_prod_ready", on)
                x_ready = sem(f"{name}_x_ready", on)
                counted = sem(f"{name}_counted", on)
                stored = sem(f"{name}_stored", on)

                with nc.Block() as block:
                    @block.tensor
                    def _(pe):
                        def turn(g, par):
                            pe.wait_ge(xn_ready, g + 1)
                            if some(3 * g):
                                pe.wait_ge(xnt_ready, 3 * g)
                            for c in range(CC):
                                for t in range(GT):
                                    ins = pe.transpose(ps_t[c][:, t * P:(t + 1) * P],
                                                       xn[:, par, t, c * P:(c + 1) * P], ident[:])
                                ins.then_inc(t_ready, 1)

                        def batch(i):
                            for j in range(GB):
                                g, par = i * GB + j, j % 2
                                pe.wait_ge(mix_ready, 4 * (g + 1))
                                if some(CC * g):
                                    pe.wait_ge(relu_ready, CC * g)
                                for m in range(CC):
                                    for c in range(CC):
                                        ins = pe.matmul(ps_k[m][:], w_k[:, c, m * P:(m + 1) * P],
                                                        xk[:, par, c, :], start=(c == 0), stop=(c == CC - 1))
                                    ins.then_inc(k_ready, 1)
                                if not (isinstance(i, int) and i == B - 1 and j == GB - 1):
                                    turn(g + 1, 1 - par)
                                for pair in range(2):
                                    if some(2 * g + pair - 1):
                                        pe.wait_ge(gate_ready, 2 * g + pair - 1)
                                    for t in range(2 * pair, 2 * pair + 2):
                                        for c in range(CC):
                                            ins = pe.matmul(ps_r[pair][:, (t % 2) * C:(t % 2 + 1) * C],
                                                            xr[:, par, c, t * P:(t + 1) * P], w_r[:, c, :],
                                                            start=(c == 0), stop=(c == CC - 1))
                                    ins.then_inc(r_ready, 1)
                                pe.wait_ge(kact_ready, g + 1)
                                for pair in range(2):
                                    if some(2 * g + pair - 1):
                                        pe.wait_ge(prod_ready, 2 * g + pair - 1)
                                    for t in range(2 * pair, 2 * pair + 2):
                                        for c in range(CC):
                                            ins = pe.matmul(ps_o[pair][:, (t % 2) * C:(t % 2 + 1) * C],
                                                            kact[:, c, t * P:(t + 1) * P], w_v[:, c, :],
                                                            start=(c == 0), stop=(c == CC - 1))
                                    ins.then_inc(o_ready, 1)

                        turn(0, 0)
                        looped(pe, B, batch)

                    @block.scalar
                    def _(act):
                        def normalize(g, par):
                            if some(CC * (g - 1)):
                                act.wait_ge(t_ready, CC * (g - 1))
                            for t in range(GT):
                                tile = g * GT + t
                                ins = act.activation(xn[:, par, t:t + 1, :], x_all[:, bass.ds(tile, 1), :], ACT.Identity,
                                                     bias=shift[:, bass.ds(tile, 1)], scale=rstd[:, bass.ds(tile, 1)])
                            ins.then_inc(xn_ready, 1)

                        def batch(i):
                            for j in range(GB):
                                g = i * GB + j
                                if not (isinstance(i, int) and i == B - 1 and j >= GB - 1):
                                    normalize(g + 1, (j + 1) % 2)
                                for m in range(CC):
                                    act.wait_ge(k_ready, CC * g + m + 1)
                                    if some(g):
                                        act.wait_ge(kact_ready, g)
                                    act.activation(relu[:, m, :], ps_k[m][:], ACT.Relu).then_inc(relu_ready, 1)
                                for pair in range(2):
                                    act.wait_ge(r_ready, 2 * g + pair + 1)
                                    if some(2 * g + pair - 1):
                                        act.wait_ge(prod_ready, 2 * g + pair - 1)
                                    act.activation(gate[:, pair, :], ps_r[pair][:], ACT.Tanh,
                                                   scale=0.5).then_inc(gate_ready, 1)

                        normalize(0, 0)
                        looped(act, B, batch)

                    @block.gpsimd
                    def _(pool):
                        def batch(i):
                            for j in range(GB):
                                g = i * GB + j
                                pool.wait_ge(relu_ready, CC * (g + 1))
                                if some(2 * g):
                                    pool.wait_ge(o_ready, 2 * g)
                                pool.tensor_tensor(kact[:], relu[:], relu[:], ALU.mult).then_inc(kact_ready, 1)

                        looped(pool, B, batch)

                    @block.vector
                    def _(dve):
                        def mix(g, par, first):
                            if some(2 * (g - 1)):
                                dve.wait_ge(r_ready, 2 * (g - 1))
                            if first:
                                dve.memset(xnt[:, par, :, 0:1], 0.0).then_inc(xnt_ready, 1)
                            else:
                                dve.tensor_copy(xnt[:, par, :, 0:1], xnt[:, 1 - par, :, W:W + 1]).then_inc(xnt_ready, 1)
                            for c in range(CC):
                                dve.wait_ge(t_ready, CC * g + c + 1)
                                dve.tensor_copy(xnt[:, par, c, 1:1 + W], ps_t[c][:]).then_inc(xnt_ready, 1)
                            dve.wait_ge(xnt_ready, 3 * (g + 1))
                            if some(4 * g):
                                dve.wait_ge(mix_ready, 4 * g)
                            dve.tensor_tensor(diff[:], xnt[:, par, :, 1:1 + W], xnt[:, par, :, 0:W],
                                              ALU.subtract).then_inc(diff_ready, 1)
                            dve.wait_ge(diff_ready, g + 1)
                            for dst, mu in ((xk, mu_kt), (xr, mu_rt)):
                                for c in range(CC):
                                    dve.scalar_tensor_tensor(out=dst[:, par, c, :], in0=diff[:, c, :],
                                                             scalar=mu[:, c:c + 1], in1=xnt[:, par, c, 0:W],
                                                             op0=ALU.mult, op1=ALU.add).then_inc(mix_ready, 1)

                        def batch(i):
                            for j in range(GB):
                                g = i * GB + j
                                if not (isinstance(i, int) and i == B - 1 and j == GB - 1):
                                    mix(g + 1, (j + 1) % 2, j == GB - 1)
                                for pair in range(2):
                                    n = 2 * g + pair
                                    tile = n * 2
                                    dve.wait_ge(gate_ready, n + 1)
                                    dve.wait_ge(o_ready, n + 1)
                                    if some(n - 1):
                                        dve.wait_ge(x_ready, n - 1)
                                    dve.scalar_tensor_tensor(
                                        out=prod[:, pair, :, :], in0=gate[:, pair, :].rearrange("p (t c) -> p t c", t=2),
                                        scalar=1.0, in1=ps_o[pair][:].rearrange("p (t c) -> p t c", t=2),
                                        op0=ALU.add, op1=ALU.mult).then_inc(prod_ready, 1)
                                    dve.wait_ge(prod_ready, n + 1)
                                    here = x_all[:, bass.ds(tile, 2), :]
                                    dve.scalar_tensor_tensor(out=here, in0=prod[:, pair, :, :], scalar=0.25, in1=here,
                                                             op0=ALU.mult, op1=ALU.add).then_inc(x_ready, 1)
                                    if not last:
                                        dve.wait_ge(x_ready, n + 1)
                                        for t in range(2):
                                            dve.bn_stats(stats[:, bass.ds(tile + t, 1), :],
                                                         x_all[:, bass.ds(tile + t, 1), :]).then_inc(counted, 1)

                        mix(0, 0, True)
                        looped(dve, B, batch)
                        dve.wait_ge(x_ready, 2 * G)
                        if not last:
                            dve.wait_ge(counted, T)

                    if last:
                        @block.sync
                        def _(sp):
                            with sp.Fori(0, G) as g:
                                tile = snap(sp, g * GT)
                                sp.wait_ge(x_ready, 2 * g + 2)
                                sp.dma_start(out_tiles[:, bass.ds(tile, GT), :],
                                             x_all[:, bass.ds(tile, GT), :]).then_inc(stored, 16)
                            sp.wait_ge(stored, 16 * G)

        ffn("ffn1", False)

        v_all = sb("v_all", [P, T, C], F32)

        ln_scalars("attn_ln")
        with ExitStack() as on:
            table = sb("table", [P, 2, 2, W], F32, on)
            xn = sb("a_xn", [P, 2, GT, C], F32, on)
            xnt = sb("a_xnt", [P, 2, CC, W], F32, on)
            qk = sb("qk", [P, 2, 2, CC, W], F32, on)
            swapped = sb("swapped", [P, 2, CC, W], F32, on)
            part = sb("part", [P, 2, PARTS, CC, W], BF16, on)
            ps_t = [ps(f"a_ps_t{c}", [P, W], F32, on) for c in range(CC)]
            ps_q = [ps(f"a_ps_q{c}", [P, W], F32, on) for c in range(2 * CC)]
            ps_v = [ps(f"a_ps_v{c}", [P, 2 * C], F32, on) for c in range(2)]
            tab_loaded = [sem(f"tab_loaded{a}", on) for a in range(2)]
            xn_ready = sem("a_xn_ready", on)
            t_ready = sem("a_t_ready", on)
            xnt_ready = sem("a_xnt_ready", on)
            q_ready = sem("q_ready", on)
            qk_ready = sem("qk_ready", on)
            swap_in = [sem(f"swap_in{a}", on) for a in range(2)]
            turned = sem("turned", on)
            rope_ready = sem("rope_ready", on)
            high_ready = sem("high_ready", on)
            rest_ready = sem("rest_ready", on)
            mid_ready = sem("mid_ready", on)
            low_ready = sem("low_ready", on)
            sent = [sem(f"sent{a}", on) for a in range(2)]
            v_ready = sem("a_v_ready", on)
            v_kept = sem("v_kept", on)

            def last_step(i, j):
                return isinstance(i, int) and i == B - 1 and j == GB - 1

            def first_step(i, j):
                return isinstance(i, int) and i == 0 and j == 0

            with nc.Block() as block:
                @block.sync
                def _(sp):
                    def load_table(g, j):
                        used = snap(sp, 4 * CC * (g - 1))
                        if some(used):
                            sp.wait_ge(turned, used)
                        for f, src in enumerate((cos, sin)):
                            sp.dma_start(table[:, j % 2, f, :], src[:, j * W:(j + 1) * W]).then_inc(tab_loaded[j % 2], 16)

                    def swap(g, par, a):
                        made, used = snap(sp, CC * (2 * g + a + 1)), snap(sp, 2 * (g - 1) + a + 1)
                        sp.wait_ge(qk_ready, made)
                        if some(used):
                            sp.wait_ge(rope_ready, used)
                        for odd in range(2):
                            sp.dma_start(swapped[odd::2, a, :, :], qk[1 - odd::2, par, a, :, :]).then_inc(swap_in[a], 16)

                    def send(g, a):
                        sp.wait_ge(low_ready, 2 * g + a + 1)
                        for s in range(PARTS):
                            sp.dma_start(split_dram[a, s, :, bass.ds(g * W, W)].rearrange("(c p) n -> p c n", p=P),
                                         part[:, a, s, :, :]).then_inc(sent[a], 16)

                    def batch(i):
                        for j in range(GB):
                            g = i * GB + j
                            for a in range(2):
                                swap(g, j % 2, a)
                            if not last_step(i, j):
                                load_table(g + 1, (j + 1) % GB)
                            if not first_step(i, j):
                                for a in range(2):
                                    send(g - 1, a)

                    load_table(0, 0)
                    looped(sp, B, batch)
                    for a in range(2):
                        send(G - 1, a)
                    for a in range(2):
                        sp.wait_ge(sent[a], 16 * PARTS * G)

                @block.tensor
                def _(pe):
                    def turn(g, par):
                        pe.wait_ge(xn_ready, g + 1)
                        if some(CC * g):
                            pe.wait_ge(xnt_ready, CC * g)
                        for c in range(CC):
                            for t in range(GT):
                                ins = pe.transpose(ps_t[c][:, t * P:(t + 1) * P],
                                                   xn[:, par, t, c * P:(c + 1) * P], ident[:])
                            ins.then_inc(t_ready, 1)

                    def batch(i):
                        for j in range(GB):
                            g, par = i * GB + j, j % 2
                            pe.wait_ge(xnt_ready, CC * (g + 1))
                            for m in range(2 * CC):
                                if some(2 * CC * (g - 1) + m + 1):
                                    pe.wait_ge(qk_ready, 2 * CC * (g - 1) + m + 1)
                                for c in range(CC):
                                    ins = pe.matmul(ps_q[m][:], w_qkv[:, c, m * P:(m + 1) * P], xnt[:, par, c, :],
                                                    start=(c == 0), stop=(c == CC - 1))
                                ins.then_inc(q_ready, 1)
                                if m == CC - 1 and not last_step(i, j):
                                    turn(g + 1, 1 - par)
                            for pair in range(2):
                                if some(2 * g + pair - 1):
                                    pe.wait_ge(v_kept, 2 * g + pair - 1)
                                for t in range(2 * pair, 2 * pair + 2):
                                    for c in range(CC):
                                        ins = pe.matmul(ps_v[pair][:, (t % 2) * C:(t % 2 + 1) * C],
                                                        xnt[:, par, c, t * P:(t + 1) * P], w_qkv[:, c, 2 * C:3 * C],
                                                        start=(c == 0), stop=(c == CC - 1))
                                ins.then_inc(v_ready, 1)

                    turn(0, 0)
                    looped(pe, B, batch)

                @block.scalar
                def _(act):
                    def normalize(g, par):
                        if some(CC * (g - 1)):
                            act.wait_ge(t_ready, CC * (g - 1))
                        for t in range(GT):
                            tile = g * GT + t
                            ins = act.activation(xn[:, par, t:t + 1, :], x_all[:, bass.ds(tile, 1), :], ACT.Identity,
                                                 bias=shift[:, bass.ds(tile, 1)], scale=rstd[:, bass.ds(tile, 1)])
                        ins.then_inc(xn_ready, 1)

                    def take(g, par, a):
                        if some(2 * (g - 2) + a + 1):
                            act.wait_ge(low_ready, 2 * (g - 2) + a + 1)
                        for c in range(CC):
                            m = a * CC + c
                            act.wait_ge(q_ready, 2 * CC * g + m + 1)
                            act.activation(qk[:, par, a, c, :], ps_q[m][:], ACT.Identity,
                                           bias=b_qk[:, m:m + 1]).then_inc(qk_ready, 1)

                    def high(g, par, a):
                        act.wait_ge(rope_ready, 2 * g + a + 1)
                        if some(16 * PARTS * g):
                            act.wait_ge(sent[a], 16 * PARTS * g)
                        act.activation(part[:, a, 0, :, :], qk[:, par, a, :, :], ACT.Copy).then_inc(high_ready, 1)

                    def mid(g, par, a):
                        act.wait_ge(rest_ready, 2 * g + a + 1)
                        act.activation(part[:, a, 1, :, :], qk[:, par, a, :, :], ACT.Copy).then_inc(mid_ready, 1)

                    def batch(i):
                        for j in range(GB):
                            g, par = i * GB + j, j % 2
                            for a in range(2):
                                take(g, par, a)
                                if not first_step(i, j):
                                    high(g - 1, 1 - par, a)
                            if not (isinstance(i, int) and i == B - 1 and j >= GB - 2):
                                normalize(g + 2, par)
                            if not first_step(i, j):
                                for a in range(2):
                                    mid(g - 1, 1 - par, a)

                    normalize(0, 0)
                    normalize(1, 1)
                    looped(act, B, batch)
                    for split_step in (high, mid):
                        for a in range(2):
                            split_step(G - 1, 1, a)

                @block.gpsimd
                def _(pool):
                    def products(g, j, n_before):
                        par = j % 2
                        pool.wait_ge(tab_loaded[par], 32 * (n_before + 1))
                        for a in range(2):
                            for c in range(CC):
                                if c == 0:
                                    pool.wait_ge(swap_in[a], 32 * (g + 1))
                                for row, f in ((qk[:, par, a, c, :], 0), (swapped[:, a, c, :], 1)):
                                    pool.tensor_tensor(row, row, table[:, par, f, :], ALU.mult).then_inc(turned, 1)

                    def batch(i):
                        for j in range(GB):
                            if not first_step(i, j):
                                before = (j - 1) % GB
                                n = i * GB + j - 1
                                n_before = i * (GB // 2) + (before // 2 if j else -1)
                                products(n, before, n_before)

                    looped(pool, B, batch)
                    products(G - 1, GB - 1, G // 2 - 1)

                @block.vector
                def _(dve):
                    def take_turned(g, par):
                        if some(2 * (g - 1)):
                            dve.wait_ge(v_ready, 2 * (g - 1))
                        for c in range(CC):
                            dve.wait_ge(t_ready, CC * g + c + 1)
                            dve.tensor_copy(xnt[:, par, c, :], ps_t[c][:]).then_inc(xnt_ready, 1)

                    def rope(g, par, a):
                        dve.wait_ge(turned, 2 * CC * (2 * g + a + 1))
                        dve.tensor_tensor(qk[:, par, a, :, :], qk[:, par, a, :, :], swapped[:, a, :, :],
                                          ALU.add).then_inc(rope_ready, 1)

                    def rest(g, par, a):
                        dve.wait_ge(high_ready, 2 * g + a + 1)
                        dve.tensor_tensor(qk[:, par, a, :, :], qk[:, par, a, :, :], part[:, a, 0, :, :],
                                          ALU.subtract).then_inc(rest_ready, 1)

                    def low(g, par, a):
                        dve.wait_ge(mid_ready, 2 * g + a + 1)
                        dve.tensor_tensor(part[:, a, 2, :, :], qk[:, par, a, :, :], part[:, a, 1, :, :],
                                          ALU.subtract).then_inc(low_ready, 1)

                    def keep_v(g, pair):
                        dve.wait_ge(v_ready, 2 * g + pair + 1)
                        for t in range(2):
                            tile = g * GT + 2 * pair + t
                            ins = dve.tensor_tensor(v_all[:, bass.ds(tile, 1), :].rearrange("p t c -> p (t c)"),
                                                    ps_v[pair][:, t * C:(t + 1) * C], b_v[:], ALU.add)
                        ins.then_inc(v_kept, 1)

                    def batch(i):
                        for j in range(GB):
                            g, par = i * GB + j, j % 2
                            if not first_step(i, j):
                                for a in range(2):
                                    rope(g - 1, 1 - par, a)
                            if not last_step(i, j):
                                take_turned(g + 1, 1 - par)
                            if not first_step(i, j):
                                for a in range(2):
                                    rest(g - 1, 1 - par, a)
                            for a in range(2):
                                keep_v(g, a)
                                if not first_step(i, j):
                                    low(g - 1, 1 - par, a)

                    take_turned(0, 0)
                    looped(dve, B, batch)
                    for split_step in (rope, rest, low):
                        for a in range(2):
                            split_step(G - 1, 1, a)
                    dve.wait_ge(v_kept, 2 * G)

        with ExitStack() as on:
            LEAD = TB + TB // 4
            SLOTS = HEADS * TB
            q_a = sb("q_a", [R, 2, N], BF16, on)
            k_a = sb("k_a", [R, 2, N], BF16, on)
            q_b = sb("q_b", [R + PARTS, 2, N], BF16, on)
            k_b = sb("k_b", [R + PARTS, 2, N], BF16, on)
            probs = sb("probs", [P, 2, N], F32, on)
            VW = 2 * D
            v_h = sb("v_h", [P, 2, TB, VW], F32, on)
            half_max = sb("half_max", [P, 2, TB, 2], F32, on)
            neg_max = sb("neg_max", [P, TB], F32, on)
            max_part = sb("max_part", [P, PARTS, TB], BF16, on)
            max_rows = sb("max_rows", [PARTS * TB, P], BF16, on)
            o_t = sb("o_t", [P, W], F32, on)
            recip = sb("recip", [P, NJ, NJ], F32, on)
            ps_e = [ps(f"ps_e{n}", [P, W], F32, on) for n in range(2)]
            ps_m = [ps(f"ps_m{n}", [P, 2, W], F32, on) for n in range(2)]
            ps_o = ps("ps_o", [P, W], F32, on)
            ps_x = ps("ps_x", [P, W], F32, on)

            def head_slice(h):
                return v_all[:, bass.ds(h // H * TB, TB), bass.ds(h % H * D, D)]

            ones_ready = sem("ones_ready", on)
            a_loaded = sem("a_loaded", on)
            b_loaded = sem("b_loaded", on)
            m_loaded = sem("m_loaded", on)
            v_copied = sem("v_copied", on)
            e_ready = sem("e_ready", on)
            exp_done = sem("exp_done", on)
            s_ready = sem("s_ready", on)
            max_done = sem("max_done", on)
            split = sem("split", on)
            rows_ready = sem("rows_ready", on)
            rows_taken = sem("rows_taken", on)
            pv_done = sem("pv_done", on)
            o_taken = sem("o_taken", on)
            o_turned = sem("o_turned", on)
            recip_done = sem("recip_done", on)
            o_kept = sem("o_kept", on)

            with nc.Block() as block:
                @block.sync
                def _(sp):
                    def load_a(h, par):
                        row, col = h % H * D, h // H * N
                        row, col = snap(sp, row), snap(sp, col)
                        made, copied = snap(sp, 2 * TB * (h - 1)), snap(sp, 32 * (h - 1))
                        if some(made):
                            sp.wait_ge(s_ready, made)
                        if some(copied):
                            sp.wait_ge(b_loaded, copied)
                        for n, (a, b) in enumerate(PAIRS):
                            for side, s, dst in ((0, a, q_a), (1, b, k_a)):
                                src = split_dram[side, s, bass.ds(row, D), bass.ds(col, N)]
                                sp.dma_start(dst[n * D:(n + 1) * D, par, :], src).then_inc(a_loaded, 16)

                    def copy_b(h, par):
                        loaded, copied = snap(sp, 32 * len(PAIRS) * (h + 1)), snap(sp, 32 * h)
                        used = snap(sp, NJ * TB * (h - 1))
                        sp.wait_ge(a_loaded, loaded)
                        if some(copied):
                            sp.wait_ge(b_loaded, copied)
                        if some(used):
                            sp.wait_ge(e_ready, used)
                        sp.dma_start(q_b[0:R, par, :], q_a[:, par, :]).then_inc(b_loaded, 16)
                        sp.dma_start(k_b[0:R, par, :], k_a[:, par, :]).then_inc(b_loaded, 16)

                    def load_max(h, par):
                        sp.wait_ge(rows_taken, h + 1)
                        sp.dma_start(q_b[R:R + PARTS, par, :], max_rows[:]).then_inc(m_loaded, 16)

                    def two_heads(i):
                        for e in range(2):
                            h = 2 * i + e + 1
                            if isinstance(i, int) and h >= HEADS:
                                continue
                            copy_b(h, (e + 1) % 2)
                            if not (isinstance(i, int) and h + 1 >= HEADS):
                                load_a(h + 1, e)
                            load_max(h, (e + 1) % 2)

                    load_a(0, 0)
                    copy_b(0, 0)
                    load_a(1, 1)
                    load_max(0, 0)
                    looped(sp, HEADS // 2, two_heads)

                @block.gpsimd
                def _(pool):
                    pool.memset(v_h[:], 1.0).then_inc(ones_ready, 1)
                    pool.wait_ge(ones_ready, 1)
                    pool.memset(k_b[R:R + PARTS, :, :], 1.0).then_inc(ones_ready, 1)
                    pool.wait_ge(ones_ready, 2)

                    def two_heads(i):
                        for e in range(2):
                            h = 2 * i + e
                            if some(TB * (h - 1)):
                                pool.wait_ge(pv_done, TB * (h - 1))
                            pool.tensor_copy(v_h[:, e, :, 0:D], head_slice(h)).then_inc(v_copied, 1)

                    looped(pool, HEADS // 2, two_heads)

                @block.tensor
                def _(pe):
                    def score_max(m, j, par, t):
                        if j % 2 == 0:
                            if some(2 * m + j // 2 - 1):
                                pe.wait_ge(max_done, 2 * m + j // 2 - 1)
                        ins = pe.matmul(ps_m[j // 2][:, j % 2, :], q_a[:, par, t * P:(t + 1) * P],
                                        k_a[:, par, j * W:(j + 1) * W], start=True, stop=True)
                        if j % 2 == 1:
                            ins.then_inc(s_ready, 1)

                    def turn_max(h):
                        pe.wait_ge(split, 5 * (h + 1))
                        if some(h - 1):
                            pe.wait_ge(o_kept, h - 1)
                        pe.matmul(ps_x[0:PARTS * TB, 0:P], max_part[:].rearrange("p s t -> p (s t)"), ident_b[:],
                                  start=True, stop=True).then_inc(rows_ready, 1)

                    def turn_out(h):
                        pe.wait_ge(o_taken, h + 1)
                        pe.wait_ge(rows_taken, h + 2)
                        for s in range(W // P):
                            ins = pe.transpose(ps_x[:, s * P:(s + 1) * P], o_t[:, s * P:(s + 1) * P], ident[:])
                        ins.then_inc(o_turned, 1)

                    def pv(k, par, kt):
                        pe.wait_ge(exp_done, NJ * (k + 1))
                        for j in range(NJ):
                            ins = pe.matmul(ps_o[VW * j:VW * (j + 1), :], v_h[:, par, kt, :],
                                            probs[:, kt % 2, j * W:(j + 1) * W], start=(kt == 0), stop=(kt == TB - 1))
                        ins.then_inc(pv_done, 1)

                    def two_heads(i):
                        for s in range(2 * TB):
                            e, kt = s // TB, s % TB
                            k = i * (2 * TB) + s
                            h = 2 * i + e
                            m = k + LEAD
                            ahead = (s + LEAD) // TB % 2
                            has_max = not (isinstance(i, int) and m >= SLOTS)
                            if kt == 0:
                                pe.wait_ge(b_loaded, 32 * (h + 1))
                                pe.wait_ge(m_loaded, 16 * (h + 1))
                            if has_max and (s + LEAD) % TB == 0:
                                pe.wait_ge(a_loaded, 32 * len(PAIRS) * (2 * i + (s + LEAD) // TB + 1))
                            for j0 in range(0, NJ, 2):
                                for j in (j0, j0 + 1):
                                    if some(NJ * k + j - 1):
                                        pe.wait_ge(exp_done, NJ * k + j - 1)
                                    pe.matmul(ps_e[j % 2][:], k_b[:, e, kt * P:(kt + 1) * P],
                                              q_b[:, e, j * W:(j + 1) * W], start=True, stop=True).then_inc(e_ready, 1)
                                if has_max and j0 == 0:
                                    for j in range(NJ):
                                        score_max(m, j, ahead, (s + LEAD) % TB)
                            if kt == 3 and not (isinstance(i, int) and h == 0):
                                turn_out(h - 1)
                            if kt == 13 and not (isinstance(i, int) and h + 1 >= HEADS):
                                turn_max(h + 1)
                            if kt == 0:
                                if not (isinstance(i, int) and h == 0):
                                    pv(k - 1, 1 - e, TB - 1)
                            else:
                                if kt == 1:
                                    pe.wait_ge(v_copied, h + 1)
                                    if some(h):
                                        pe.wait_ge(o_taken, h)
                                pv(k - 1, e, kt - 1)

                    for m in range(LEAD):
                        if m % TB == 0:
                            pe.wait_ge(a_loaded, 32 * len(PAIRS) * (m // TB + 1))
                        for j in range(NJ):
                            score_max(m, j, m // TB, m % TB)
                    turn_max(0)
                    pe.wait_ge(ones_ready, 2)
                    looped(pe, HEADS // 2, two_heads)
                    pv(SLOTS - 1, 1, TB - 1)
                    pe.wait_ge(o_taken, HEADS)
                    pe.wait_ge(o_kept, HEADS - 1)
                    for s in range(W // P):
                        ins = pe.transpose(ps_x[:, s * P:(s + 1) * P], o_t[:, s * P:(s + 1) * P], ident[:])
                    ins.then_inc(o_turned, 1)

                @block.scalar
                def _(act):
                    def take_rows(h):
                        act.wait_ge(rows_ready, h + 1)
                        if some(16 * h):
                            act.wait_ge(m_loaded, 16 * h)
                        act.activation(max_rows[:], ps_x[0:PARTS * TB, 0:P], ACT.Copy).then_inc(rows_taken, 1)

                    def take_out(h):
                        act.wait_ge(pv_done, TB * (h + 1))
                        if some(h):
                            act.wait_ge(o_turned, h)
                        act.activation(o_t[:], ps_o[:], ACT.Copy).then_inc(o_taken, 1)

                    def two_heads(i):
                        for s in range(2 * TB):
                            e, kt = s // TB, s % TB
                            k = i * (2 * TB) + s
                            h = 2 * i + e
                            for j in range(NJ):
                                act.wait_ge(e_ready, NJ * k + j + 1)
                                if j == 0:
                                    if some(k - 1):
                                        act.wait_ge(pv_done, k - 1)
                                act.activation(probs[:, kt % 2, j * W:(j + 1) * W], ps_e[j % 2][:], ACT.Exp,
                                               scale=scale).then_inc(exp_done, 1)
                            if kt == 0 and not (isinstance(i, int) and h == 0):
                                take_out(h - 1)
                            if kt == 13 and not (isinstance(i, int) and h + 1 >= HEADS):
                                take_rows(h + 1)

                    take_rows(0)
                    looped(act, HEADS // 2, two_heads)
                    take_out(HEADS - 1)

                @block.vector
                def _(dve):
                    def slot_max(m, par, t):
                        for half in range(2):
                            dve.wait_ge(s_ready, 2 * m + half + 1)
                            dve.tensor_reduce(half_max[:, par, t, half:half + 1], ps_m[half][:], AX.XY,
                                              ALU.max).then_inc(max_done, 1)

                    def split_max(h, par):
                        dve.wait_ge(max_done, 2 * TB * (h + 1))
                        dve.tensor_reduce(neg_max[:], half_max[:, par, :, :], AX.X, ALU.max,
                                          negate=True).then_inc(split, 1)
                        if some(h):
                            dve.wait_ge(rows_ready, h)
                        for s in range(PARTS - 1):
                            dve.wait_ge(split, 5 * h + 2 * s + 1)
                            dve.tensor_copy(max_part[:, s, :], neg_max[:]).then_inc(split, 1)
                            dve.wait_ge(split, 5 * h + 2 * s + 2)
                            rest = neg_max[:] if s < PARTS - 2 else max_part[:, PARTS - 1, :]
                            dve.tensor_tensor(rest, neg_max[:], max_part[:, s, :], ALU.subtract).then_inc(split, 1)

                    def keep_out(h):
                        dve.wait_ge(o_turned, h + 1)
                        turned = ps_x[:].rearrange("p (s j d) -> p s j d", j=NJ, d=VW)
                        if some(h):
                            dve.wait_ge(o_kept, h)
                        dve.reciprocal(recip[:], turned[:, :, :, D]).then_inc(recip_done, 1)
                        dve.wait_ge(recip_done, h + 1)
                        dst = head_slice(h).rearrange("p (j s) d -> p s j d", j=NJ)
                        dve.tensor_tensor(dst, turned[:, :, :, 0:D],
                                          recip[:].rearrange("p s (j o) -> p s j o", o=1).broadcast_to([P, NJ, NJ, D]),
                                          ALU.mult).then_inc(o_kept, 1)

                    def two_heads(i):
                        for s in range(2 * TB):
                            e, kt = s // TB, s % TB
                            k = i * (2 * TB) + s
                            h = 2 * i + e
                            if not (isinstance(i, int) and k + LEAD >= SLOTS):
                                slot_max(k + LEAD, (s + LEAD) // TB % 2, (s + LEAD) % TB)
                            if kt == 11 and not (isinstance(i, int) and h + 1 >= HEADS):
                                split_max(h + 1, 1 - e)
                            if kt == 4 and not (isinstance(i, int) and h == 0):
                                keep_out(h - 1)

                    for m in range(LEAD):
                        slot_max(m, m // TB, m % TB)
                        if m == TB - 1:
                            split_max(0, 0)
                    looped(dve, HEADS // 2, two_heads)
                    keep_out(HEADS - 1)
                    dve.wait_ge(o_kept, HEADS)

        with ExitStack() as on:
            attn = sb("attn", [P, 2, GT, C], F32, on)
            attn_t = sb("attn_t", [P, 2, CC, W], F32, on)
            ps_t = [ps(f"p_ps_t{c}", [P, W], F32, on) for c in range(2 * CC)]
            ps_y = [ps(f"p_ps_y{c}", [P, 2, C], F32, on) for c in range(2)]
            attn_ready = sem("attn_ready", on)
            t_ready = sem("p_t_ready", on)
            attn_t_ready = sem("attn_t_ready", on)
            y_ready = sem("y_ready", on)
            sum_ready = sem("sum_ready", on)
            x_ready = sem("p_x_ready", on)
            counted = sem("p_counted", on)

            with nc.Block() as block:
                @block.gpsimd
                def _(pool):
                    def batch(i):
                        for j in range(GB):
                            g = i * GB + j
                            if some(CC * (g - 1)):
                                pool.wait_ge(t_ready, CC * (g - 1))
                            pool.tensor_copy(attn[:, j % 2, :, :], v_all[:, bass.ds(g * GT, GT), :]).then_inc(attn_ready, 1)

                    looped(pool, B, batch)

                @block.tensor
                def _(pe):
                    def turn(g, par):
                        pe.wait_ge(attn_ready, g + 1)
                        if some(CC * (g - 1)):
                            pe.wait_ge(attn_t_ready, CC * (g - 1))
                        for c in range(CC):
                            for t in range(GT):
                                ins = pe.transpose(ps_t[par * CC + c][:, t * P:(t + 1) * P],
                                                   attn[:, par, t, c * P:(c + 1) * P], ident[:])
                            ins.then_inc(t_ready, 1)

                    def batch(i):
                        for j in range(GB):
                            g, par = i * GB + j, j % 2
                            if not (isinstance(i, int) and i == B - 1 and j == GB - 1):
                                turn(g + 1, 1 - par)
                            pe.wait_ge(attn_t_ready, CC * (g + 1))
                            for pair in range(2):
                                if some(2 * g + pair - 1):
                                    pe.wait_ge(sum_ready, 2 * g + pair - 1)
                                for t in range(2 * pair, 2 * pair + 2):
                                    for c in range(CC):
                                        ins = pe.matmul(ps_y[pair][:, t % 2, :], attn_t[:, par, c, t * P:(t + 1) * P],
                                                        w_proj[:, c, :], start=(c == 0), stop=(c == CC - 1))
                                ins.then_inc(y_ready, 1)

                    turn(0, 0)
                    looped(pe, B, batch)

                @block.scalar
                def _(act):
                    def batch(i):
                        for j in range(GB):
                            g, par = i * GB + j, j % 2
                            if some(2 * (g - 1)):
                                act.wait_ge(y_ready, 2 * (g - 1))
                            for c in range(CC):
                                act.wait_ge(t_ready, CC * g + c + 1)
                                act.activation(attn_t[:, par, c, :], ps_t[par * CC + c][:],
                                               ACT.Copy).then_inc(attn_t_ready, 1)

                    looped(act, B, batch)

                @block.vector
                def _(dve):
                    def batch(i):
                        for n0 in range(2 * GB):
                            n, pair = i * 2 * GB + n0, n0 % 2
                            here = x_all[:, bass.ds(2 * n, 2), :]
                            dve.wait_ge(y_ready, n + 1)
                            dve.tensor_tensor(here, here, ps_y[pair][:], ALU.add).then_inc(sum_ready, 1)
                            dve.wait_ge(sum_ready, n + 1)
                            dve.tensor_tensor(here, here, b_proj[:].rearrange("p (o c) -> p o c", o=1)
                                              .broadcast_to([P, 2, C]), ALU.add).then_inc(x_ready, 1)
                            dve.wait_ge(x_ready, n + 1)
                            for t in range(2):
                                dve.bn_stats(stats[:, bass.ds(2 * n + t, 1), :],
                                             x_all[:, bass.ds(2 * n + t, 1), :]).then_inc(counted, 1)

                    looped(dve, B, batch)
                    dve.wait_ge(counted, T)

        ffn("ffn2", True)


def kernel(L0_attn_x, L0_attn_qkv_w, L0_attn_qkv_b, L0_attn_proj_w, L0_attn_proj_b, L0_ffn_W_r, L0_ffn_W_k,
           L0_ffn_W_v, L0_ffn_mu_r, L0_ffn_mu_k):
    import numpy as np
    import concourse.bacc as bacc
    from concourse.bass_utils import run_bass_kernel_spmd

    B, N, C = L0_attn_x.shape
    D = C // 16
    inv = np.float32(1.0) / np.float32(10000.0) ** (np.arange(0, D, 2, dtype=np.float32) / np.float32(D))
    angle = np.arange(N, dtype=np.float32)[None, :] * inv.astype(np.float32)[:, None]
    rows = (np.arange(P) % D) // 2
    sign = np.where(np.arange(P) % 2 == 0, -1.0, 1.0).astype(np.float32)[:, None]

    def columns(v):
        return np.asarray(v).reshape(-1, P).T

    arrays = {
        "x": L0_attn_x, "wr_t": L0_ffn_W_r.T, "wk_t": L0_ffn_W_k.T, "wv_t": L0_ffn_W_v.T,
        "mu_r": columns(L0_ffn_mu_r), "mu_k": columns(L0_ffn_mu_k),
        "qkv_t": L0_attn_qkv_w.T, "qk_b": columns(L0_attn_qkv_b[:2 * C]), "qkv_b": L0_attn_qkv_b,
        "proj_t": L0_attn_proj_w.T, "proj_b": L0_attn_proj_b,
        "cos": np.cos(angle)[rows], "sin": np.sin(angle)[rows] * sign,
    }
    arrays = {f"in_{k}": np.ascontiguousarray(np.asarray(v)) for k, v in arrays.items()}
    nc = bacc.Bacc("TRN2", target_bir_lowering=False, num_devices=1)
    args = [nc.dram_tensor(k, v.shape, F32, kind="ExternalInput").ap() for k, v in arrays.items()]
    out = nc.dram_tensor("out_0", (B, N, C), F32, kind="ExternalOutput").ap()
    macaron(nc, *args, out)
    r = run_bass_kernel_spmd(nc, [arrays], core_ids=[0])
    return r.results[0]["out_0"]
```

```python
from contextlib import ExitStack

import concourse.bass as bass
from concourse import mybir

F32 = mybir.dt.float32
BF16 = mybir.dt.bfloat16
I32 = mybir.dt.int32
ALU = mybir.AluOpType
ACT = mybir.ActivationFunctionType
AX = mybir.AxisListType

P = 128
EPS = 1e-5
PARTS = 3
PAIRS = [(0, 0), (0, 1), (0, 2), (1, 0), (1, 1), (2, 0)]


def some(count):
    return not isinstance(count, int) or count > 0


def snap(eng, value):
    return value if isinstance(value, int) else eng.snap(eng.to_reg(value))


def looped(eng, n, step):
    step(0)
    with eng.Fori(1, n - 1) as i:
        step(i)
    step(n - 1)


def macaron(nc, x, wr_t, wk_t, wv_t, mu_r, mu_k, qkv_t, qk_b, qkv_b, proj_t, proj_b, cos, sin, out):
    B, N, C = x.shape
    H, D = 16, C // 16
    T = B * N // P
    GT = 4
    W = GT * P
    G = T // GT
    GB = G // B
    CC = C // P
    TB = T // B
    FIRST = T - TB
    HEADS = B * H
    R = len(PAIRS) * D
    NJ = N // W
    scale = float(D) ** -0.5

    x_tiles = x.rearrange("b (t p) c -> p (b t) c", p=P)
    out_tiles = out.rearrange("b (t p) c -> p (b t) c", p=P)
    split_dram = nc.dram_tensor("split_dram", (2, PARTS, C, B * N), BF16, kind="Internal").ap()

    ctx = ExitStack()
    with ctx:
        def sb(name, shape, dt, on=ctx):
            return on.enter_context(nc.sbuf_tensor(name, shape, dt))

        def ps(name, shape, dt, on):
            return on.enter_context(nc.psum_tensor(name, shape, dt))

        def sem(name, on):
            return on.enter_context(nc.semaphore(name))

        x_all = sb("x_all", [P, T, C], F32)
        ident = sb("ident", [P, P], F32)
        ident_b = sb("ident_b", [P, P], BF16)
        w_r = sb("w_r", [P, CC, C], F32)
        w_k = sb("w_k", [P, CC, C], F32)
        w_v = sb("w_v", [P, CC, C], F32)
        w_qkv = sb("w_qkv", [P, CC, 3 * C], F32)
        w_proj = sb("w_proj", [P, CC, C], F32)
        mu_rt = sb("mu_rt", [P, CC], F32)
        mu_kt = sb("mu_kt", [P, CC], F32)
        b_qk = sb("b_qk", [P, 2 * CC], F32)
        b_v = sb("b_v", [P, C], F32)
        b_proj = sb("b_proj", [P, C], F32)
        stats = sb("stats", [P, T, 6], F32)
        rstd = sb("rstd", [P, T], F32)
        shift = sb("shift", [P, T], F32)

        half = sb("half", [P, T], F32)
        mean = sb("mean", [P, T], F32)
        var = sb("var", [P, T], F32)
        root = sb("root", [P, T], F32)

        CHAIN = 10

        def var_plus_eps(dve, t0, n, chain, before, var_ready):
            at = bass.ds(t0, n)
            even, odd = stats[:, at, 1], stats[:, at, 4]
            dve.tensor_tensor(half[:, at], even, odd, ALU.subtract).then_inc(chain, 1)
            dve.tensor_tensor(mean[:, at], even, odd, ALU.add).then_inc(chain, 1)
            dve.tensor_tensor(var[:, at], stats[:, at, 2], stats[:, at, 5], ALU.add).then_inc(chain, 1)
            dve.wait_ge(chain, before + 3)
            dve.scalar_tensor_tensor(out=half[:, at], in0=half[:, at], scalar=0.25, in1=half[:, at],
                                     op0=ALU.mult, op1=ALU.mult).then_inc(chain, 1)
            dve.wait_ge(chain, before + 4)
            dve.scalar_tensor_tensor(out=var[:, at], in0=var[:, at], scalar=1.0 / C, in1=half[:, at],
                                     op0=ALU.mult, op1=ALU.add).then_inc(chain, 1)
            dve.wait_ge(chain, before + 5)
            dve.tensor_scalar(var[:, at], var[:, at], EPS, None, ALU.add).then_inc(var_ready, 1)

        def take_root(act, t0, n, var_ready, root_ready, turn):
            act.wait_ge(var_ready, turn + 1)
            act.activation(root[:, bass.ds(t0, n)], var[:, bass.ds(t0, n)], ACT.Sqrt).then_inc(root_ready, 1)

        def rstd_and_shift(dve, t0, n, chain, before, root_ready, turn, ln_ready):
            at = bass.ds(t0, n)
            dve.wait_ge(root_ready, turn + 1)
            dve.reciprocal(rstd[:, at], root[:, at]).then_inc(chain, 1)
            dve.wait_ge(chain, before + 6)
            dve.tensor_tensor(half[:, at], rstd[:, at], rstd[:, at], ALU.mult).then_inc(chain, 1)
            dve.wait_ge(chain, before + 7)
            dve.tensor_tensor(half[:, at], half[:, at], var[:, at], ALU.mult).then_inc(chain, 1)
            dve.wait_ge(chain, before + 8)
            dve.tensor_scalar(half[:, at], half[:, at], -0.5, 1.5, ALU.mult, ALU.add).then_inc(chain, 1)
            dve.wait_ge(chain, before + 9)
            dve.tensor_tensor(rstd[:, at], rstd[:, at], half[:, at], ALU.mult).then_inc(chain, 1)
            dve.wait_ge(chain, before + 10)
            dve.scalar_tensor_tensor(out=shift[:, at], in0=mean[:, at], scalar=-0.5, in1=rstd[:, at],
                                     op0=ALU.mult, op1=ALU.mult).then_inc(ln_ready, 1)

        x_loaded = sem("x_loaded", ctx)
        w_later = sem("w_later", ctx)
        stats_ready = sem("stats_ready", ctx)
        g_loaded = [sem(f"g_loaded{g}", ctx) for g in range(GB)]
        LOADED = GB // 2
        rest_var = sem("rest_var", ctx)
        rest_root = sem("rest_root", ctx)
        rest_ln = sem("rest_ln", ctx)
        rest_chain = sem("rest_chain", ctx)
        with ExitStack() as on:
            w_loaded = sem("w_loaded", on)
            zeroed = sem("zeroed", on)
            ident_ready = sem("ident_ready", on)
            var_ready = sem("l_var_ready", on)
            root_ready = sem("l_root_ready", on)
            chain = sem("l_chain", on)
            ln_ready = sem("l_ready", on)
            with nc.Block() as block:
                @block.sync
                def _(sp):
                    for g in range(GB):
                        sp.dma_start(x_all[:, g * GT:(g + 1) * GT, :],
                                     x_tiles[:, g * GT:(g + 1) * GT, :]).then_inc(g_loaded[g], 16)

                @block.scalar
                def _(act):
                    for dst, src in ((w_k, wk_t), (w_r, wr_t), (w_v, wv_t)):
                        act.dma_start(dst[:], src.rearrange("(c p) n -> p c n", p=P)).then_inc(w_loaded, 16)
                    act.dma_start(mu_rt[:], mu_r).then_inc(w_loaded, 16)
                    act.dma_start(mu_kt[:], mu_k).then_inc(w_loaded, 16)
                    take_root(act, 0, LOADED * GT, var_ready, root_ready, 0)
                    act.wait_ge(w_loaded, 16 * 5)

                @block.gpsimd
                def _(pool):
                    pool.memset(ident[:], 0.0).then_inc(zeroed, 1)
                    pool.memset(ident_b[:], 0.0).then_inc(zeroed, 1)
                    pool.wait_ge(zeroed, 2)
                    for m in (ident, ident_b):
                        pool.affine_select(out=m[:], in_=m[:], compare_op=ALU.not_equal, fill=1.0, base=0,
                                           pattern=[[-1, P]], channel_multiplier=1).then_inc(ident_ready, 1)
                    pool.wait_ge(ident_ready, 2)

                @block.vector
                def _(dve):
                    for g in range(LOADED):
                        dve.wait_ge(g_loaded[g], 16)
                        for t in range(g * GT, (g + 1) * GT):
                            dve.bn_stats(stats[:, t, :], x_all[:, t, :]).then_inc(stats_ready, 1)
                    dve.wait_ge(stats_ready, LOADED * GT)
                    var_plus_eps(dve, 0, LOADED * GT, chain, 0, var_ready)
                    rstd_and_shift(dve, 0, LOADED * GT, chain, 0, root_ready, 0, ln_ready)

        def ffn(name, last):
            with ExitStack() as on:
                xn = sb(f"{name}_xn", [P, 2, GT, C], F32, on)
                xnt = sb(f"{name}_xnt", [P, 2, CC, 1 + W], F32, on)
                diff = sb(f"{name}_diff", [P, CC, W], F32, on)
                xr = sb(f"{name}_xr", [P, 2, CC, W], F32, on)
                xk = sb(f"{name}_xk", [P, 2, CC, W], F32, on)
                relu = sb(f"{name}_relu", [P, CC, W], F32, on)
                kact = sb(f"{name}_kact", [P, CC, W], F32, on)
                gate = sb(f"{name}_gate", [P, 2, 2 * C], F32, on)
                prod = sb(f"{name}_prod", [P, 2, 2, C], F32, on)
                ps_t = [ps(f"{name}_ps_t{c}", [P, W], F32, on) for c in range(CC)]
                ps_k = [ps(f"{name}_ps_k{c}", [P, W], F32, on) for c in range(CC)]
                ps_r = [ps(f"{name}_ps_r{c}", [P, 2 * C], F32, on) for c in range(2)]
                ps_o = [ps(f"{name}_ps_o{c}", [P, 2 * C], F32, on) for c in range(2)]
                xn_ready = sem(f"{name}_xn_ready", on)
                t_ready = sem(f"{name}_t_ready", on)
                xnt_ready = sem(f"{name}_xnt_ready", on)
                prev_ready = sem(f"{name}_prev_ready", on)
                diff_ready = sem(f"{name}_diff_ready", on)
                mix_ready = sem(f"{name}_mix_ready", on)
                k_ready = sem(f"{name}_k_ready", on)
                relu_ready = sem(f"{name}_relu_ready", on)
                kact_ready = sem(f"{name}_kact_ready", on)
                r_ready = sem(f"{name}_r_ready", on)
                gate_ready = sem(f"{name}_gate_ready", on)
                o_ready = sem(f"{name}_o_ready", on)
                prod_ready = sem(f"{name}_prod_ready", on)
                x_ready = sem(f"{name}_x_ready", on)
                counted = sem(f"{name}_counted", on)
                stored = sem(f"{name}_stored", on)
                var_ready = sem(f"{name}_var_ready", on)
                root_ready = sem(f"{name}_root_ready", on)
                ln_ready = sem(f"{name}_ln_ready", on)
                chain = sem(f"{name}_chain", on)

                def last_batch(i):
                    return isinstance(i, int) and i == B - 1

                def next_tiles(i):
                    return (0, FIRST) if last_batch(i) else ((i + 1) * TB, TB)

                with nc.Block() as block:
                    @block.tensor
                    def _(pe):
                        def turn(g, par):
                            pe.wait_ge(xn_ready, g + 1)
                            if some(CC * g):
                                pe.wait_ge(xnt_ready, CC * g)
                            for c in range(CC):
                                for t in range(GT):
                                    ins = pe.transpose(ps_t[c][:, t * P:(t + 1) * P],
                                                       xn[:, par, t, c * P:(c + 1) * P], ident[:])
                                ins.then_inc(t_ready, 1)

                        def batch(i):
                            for j in range(GB):
                                g, par = i * GB + j, j % 2
                                pe.wait_ge(mix_ready, 4 * (g + 1))
                                if some(CC * g):
                                    pe.wait_ge(relu_ready, CC * g)
                                for m in range(CC):
                                    for c in range(CC):
                                        ins = pe.matmul(ps_k[m][:], w_k[:, c, m * P:(m + 1) * P],
                                                        xk[:, par, c, :], start=(c == 0), stop=(c == CC - 1))
                                    ins.then_inc(k_ready, 1)
                                if not (isinstance(i, int) and i == B - 1 and j == GB - 1):
                                    turn(g + 1, 1 - par)
                                for pair in range(2):
                                    if some(2 * g + pair - 1):
                                        pe.wait_ge(gate_ready, 2 * g + pair - 1)
                                    for t in range(2 * pair, 2 * pair + 2):
                                        for c in range(CC):
                                            ins = pe.matmul(ps_r[pair][:, (t % 2) * C:(t % 2 + 1) * C],
                                                            xr[:, par, c, t * P:(t + 1) * P], w_r[:, c, :],
                                                            start=(c == 0), stop=(c == CC - 1))
                                    ins.then_inc(r_ready, 1)
                                pe.wait_ge(kact_ready, CC * (g + 1))
                                for pair in range(2):
                                    if some(2 * g + pair - 1):
                                        pe.wait_ge(prod_ready, 2 * g + pair - 1)
                                    for t in range(2 * pair, 2 * pair + 2):
                                        for c in range(CC):
                                            ins = pe.matmul(ps_o[pair][:, (t % 2) * C:(t % 2 + 1) * C],
                                                            kact[:, c, t * P:(t + 1) * P], w_v[:, c, :],
                                                            start=(c == 0), stop=(c == CC - 1))
                                    ins.then_inc(o_ready, 1)

                        turn(0, 0)
                        looped(pe, B, batch)

                    @block.scalar
                    def _(act):
                        def normalize(g, par, rounds=None):
                            if some(CC * (g - 1)):
                                act.wait_ge(t_ready, CC * (g - 1))
                            if rounds is not None:
                                act.wait_ge(ln_ready, rounds)
                            if not last and isinstance(g, int) and g == LOADED:
                                act.wait_ge(rest_ln, 1)
                            for t in range(GT):
                                tile = g * GT + t
                                ins = act.activation(xn[:, par, t:t + 1, :], x_all[:, bass.ds(tile, 1), :], ACT.Identity,
                                                     bias=shift[:, bass.ds(tile, 1)], scale=rstd[:, bass.ds(tile, 1)])
                            ins.then_inc(xn_ready, 1)

                        def take_turned(g, par):
                            if some(4 * (g - 1)):
                                act.wait_ge(mix_ready, 4 * (g - 1))
                            for c in range(CC):
                                act.wait_ge(t_ready, CC * g + c + 1)
                                act.activation(xnt[:, par, c, 1:1 + W], ps_t[c][:], ACT.Copy).then_inc(xnt_ready, 1)

                        def batch(i):
                            for j in range(GB):
                                g = i * GB + j
                                if not (last_batch(i) and j == GB - 1):
                                    normalize(g + 1, (j + 1) % 2, None if j < GB - 1 else 1 if last else i + 1)
                                for m in range(CC):
                                    act.wait_ge(k_ready, CC * g + m + 1)
                                    if some(CC * g):
                                        act.wait_ge(kact_ready, CC * g)
                                    act.activation(relu[:, m, :], ps_k[m][:], ACT.Relu).then_inc(relu_ready, 1)
                                if some(2 * g):
                                    act.wait_ge(o_ready, 2 * g)
                                for m in range(CC):
                                    act.wait_ge(relu_ready, CC * g + m + 1)
                                    act.activation(kact[:, m, :], relu[:, m, :], ACT.Square).then_inc(kact_ready, 1)
                                if not (last_batch(i) and j == GB - 1):
                                    take_turned(g + 1, (j + 1) % 2)
                                if not last and j == 2:
                                    take_root(act, *next_tiles(i), var_ready, root_ready, i)
                                for pair in range(2):
                                    act.wait_ge(r_ready, 2 * g + pair + 1)
                                    if some(2 * g + pair - 1):
                                        act.wait_ge(prod_ready, 2 * g + pair - 1)
                                    act.activation(gate[:, pair, :], ps_r[pair][:], ACT.Tanh,
                                                   scale=0.5).then_inc(gate_ready, 1)

                        normalize(0, 0)
                        take_turned(0, 0)
                        if last:
                            take_root(act, FIRST, TB, var_ready, root_ready, 0)
                        else:
                            take_root(act, LOADED * GT, TB - LOADED * GT, rest_var, rest_root, 0)
                        looped(act, B, batch)

                    @block.gpsimd
                    def _(pool):
                        def difference(g, par):
                            if some(4 * g):
                                pool.wait_ge(mix_ready, 4 * g)
                            pool.wait_ge(prev_ready, g + 1)
                            pool.wait_ge(xnt_ready, CC * (g + 1))
                            pool.tensor_tensor(diff[:], xnt[:, par, :, 1:1 + W], xnt[:, par, :, 0:W],
                                               ALU.subtract).then_inc(diff_ready, 1)

                        def batch(i):
                            for j in range(GB):
                                g = i * GB + j
                                if not (last_batch(i) and j == GB - 1):
                                    difference(g + 1, (j + 1) % 2)

                        difference(0, 0)
                        looped(pool, B, batch)

                    @block.vector
                    def _(dve):
                        def mix(g, par, ends_batch=False, more=True):
                            if some(2 * (g - 1)):
                                dve.wait_ge(r_ready, 2 * (g - 1))
                            dve.wait_ge(diff_ready, g + 1)
                            for dst, mu in ((xk, mu_kt), (xr, mu_rt)):
                                for c in range(CC):
                                    dve.scalar_tensor_tensor(out=dst[:, par, c, :], in0=diff[:, c, :],
                                                             scalar=mu[:, c:c + 1], in1=xnt[:, par, c, 0:W],
                                                             op0=ALU.mult, op1=ALU.add).then_inc(mix_ready, 1)
                            if more:
                                dve.wait_ge(mix_ready, 4 * (g + 1))
                                after = xnt[:, 1 - par, :, 0:1]
                                if ends_batch:
                                    dve.memset(after, 0.0).then_inc(prev_ready, 1)
                                else:
                                    dve.tensor_copy(after, xnt[:, par, :, W:W + 1]).then_inc(prev_ready, 1)

                        share = TB // 2

                        def next_stats(i, j):
                            if last_batch(i):
                                if j == 1:
                                    dve.wait_ge(counted, FIRST)
                                    var_plus_eps(dve, *next_tiles(i), chain, i * CHAIN, var_ready)
                                return
                            if j == 0:
                                dve.wait_ge(x_loaded, 16 * (i + 1))
                            for t in range(j * share, min(TB, (j + 1) * share)):
                                tile = (i + 1) * TB + t
                                dve.bn_stats(stats[:, bass.ds(tile, 1), :],
                                             x_all[:, bass.ds(tile, 1), :]).then_inc(stats_ready, 1)
                            if j == 1:
                                dve.wait_ge(stats_ready, (i + 2) * TB)
                                var_plus_eps(dve, *next_tiles(i), chain, i * CHAIN, var_ready)

                        def batch(i):
                            for j in range(GB):
                                g = i * GB + j
                                if not (isinstance(i, int) and i == B - 1 and j == GB - 1):
                                    mix(g + 1, (j + 1) % 2, j == GB - 2, not (last_batch(i) and j == GB - 2))
                                if not last and j < 2:
                                    next_stats(i, j)
                                if not last and j == 2:
                                    rstd_and_shift(dve, *next_tiles(i), chain, i * CHAIN, root_ready, i, ln_ready)
                                for pair in range(2):
                                    n = 2 * g + pair
                                    tile = n * 2
                                    dve.wait_ge(gate_ready, n + 1)
                                    dve.wait_ge(o_ready, n + 1)
                                    if some(n - 1):
                                        dve.wait_ge(x_ready, n - 1)
                                    dve.scalar_tensor_tensor(
                                        out=prod[:, pair, :, :], in0=gate[:, pair, :].rearrange("p (t c) -> p t c", t=2),
                                        scalar=1.0, in1=ps_o[pair][:].rearrange("p (t c) -> p t c", t=2),
                                        op0=ALU.add, op1=ALU.mult).then_inc(prod_ready, 1)
                                    dve.wait_ge(prod_ready, n + 1)
                                    here = x_all[:, bass.ds(tile, 2), :]
                                    dve.scalar_tensor_tensor(out=here, in0=prod[:, pair, :, :], scalar=0.25, in1=here,
                                                             op0=ALU.mult, op1=ALU.add).then_inc(x_ready, 1)
                                    if not last:
                                        dve.wait_ge(x_ready, n + 1)
                                        for t in range(2):
                                            dve.bn_stats(stats[:, bass.ds(tile + t, 1), :],
                                                         x_all[:, bass.ds(tile + t, 1), :]).then_inc(counted, 1)

                        dve.memset(xnt[:, 0, :, 0:1], 0.0).then_inc(prev_ready, 1)
                        if last:
                            var_plus_eps(dve, FIRST, TB, chain, 0, var_ready)
                        mix(0, 0)
                        if last:
                            rstd_and_shift(dve, FIRST, TB, chain, 0, root_ready, 0, ln_ready)
                        else:
                            for g in range(LOADED, GB):
                                dve.wait_ge(g_loaded[g], 16)
                                for t in range(g * GT, (g + 1) * GT):
                                    dve.bn_stats(stats[:, t, :], x_all[:, t, :]).then_inc(stats_ready, 1)
                            dve.wait_ge(stats_ready, TB)
                            var_plus_eps(dve, LOADED * GT, TB - LOADED * GT, rest_chain, 0, rest_var)
                            rstd_and_shift(dve, LOADED * GT, TB - LOADED * GT, rest_chain, 0, rest_root, 0, rest_ln)
                        looped(dve, B, batch)
                        dve.wait_ge(x_ready, 2 * G)
                        if not last:
                            dve.wait_ge(counted, T)
                            dve.wait_ge(ln_ready, B)

                    if not last:
                        @block.sync
                        def _(sp):
                            for b in range(1, B):
                                if b > 1:
                                    sp.wait_ge(x_loaded, 16 * (b - 1))
                                sp.dma_start(x_all[:, b * TB:(b + 1) * TB, :],
                                             x_tiles[:, b * TB:(b + 1) * TB, :]).then_inc(x_loaded, 16)
                            for dst, src in ((w_qkv, qkv_t), (w_proj, proj_t)):
                                sp.dma_start(dst[:], src.rearrange("(c p) n -> p c n", p=P)).then_inc(w_later, 16)
                            sp.dma_start(b_qk[:], qk_b).then_inc(w_later, 16)
                            for dst, src in ((b_v, qkv_b[2 * C:3 * C]), (b_proj, proj_b)):
                                sp.dma_start(dst[:], src.rearrange("(o n) -> o n", o=1)
                                             .broadcast_to([P, C])).then_inc(w_later, 16)
                            sp.wait_ge(w_later, 16 * 5)

                    if last:
                        @block.sync
                        def _(sp):
                            with sp.Fori(0, G) as g:
                                tile = snap(sp, g * GT)
                                sp.wait_ge(x_ready, 2 * g + 2)
                                sp.dma_start(out_tiles[:, bass.ds(tile, GT), :],
                                             x_all[:, bass.ds(tile, GT), :]).then_inc(stored, 16)
                            sp.wait_ge(stored, 16 * G)

        ffn("ffn1", False)

        v_all = sb("v_all", [P, T, C], F32)

        both = ctx.enter_context(ExitStack())
        stack_a = sb("stack_a", [P, 2, 2, N], BF16, both)
        q_b = sb("q_b", [P, 2, N], BF16, both)
        k_b = sb("k_b", [P, 2, N], BF16, both)
        probs = sb("probs", [P, 2, N], F32, both)

        xn = stack_a[:, 0, :, :].bitcast(F32).rearrange("p a (t c) -> p a t c", c=C)
        xnt = stack_a[:, 1, :, :].bitcast(F32).rearrange("p a (c w) -> p a c w", w=W)
        swapped = k_b[:].bitcast(F32).rearrange("p a (c w) -> p a c w", w=W)
        odd_qk = probs[:, 0, :].rearrange("p (a c w) -> p a c w", a=2, w=W)
        odd_table = q_b[:, 0, :].bitcast(F32).rearrange("p (f w) -> p f w", w=W)
        pieces = ([probs[:, 1, n * W:(n + 1) * W].bitcast(BF16) for n in range(4)]
                  + [q_b[:, 1, n * CC * W:(n + 1) * CC * W] for n in range(2)])
        part = [[pieces[PARTS * a + s].rearrange("p (c w) -> p c w", w=W) for s in range(PARTS)] for a in range(2)]

        tab_loaded = [sem(f"tab_loaded{a}", ctx) for a in range(2)]
        swap_in = [sem(f"swap_in{a}", ctx) for a in range(2)]
        turned = sem("turned", ctx)
        rope_ready = sem("rope_ready", ctx)
        high_ready = sem("high_ready", ctx)
        rest_ready = sem("rest_ready", ctx)
        mid_ready = sem("mid_ready", ctx)
        low_ready = sem("low_ready", ctx)
        sent = [sem(f"sent{a}", ctx) for a in range(2)]
        a_loaded = sem("a_loaded", ctx)

        def rope_products(pool, g, j, n_before):
            par = j % 2
            pool.wait_ge(tab_loaded[par], 32 * (n_before + 1))
            for a in range(2):
                for c in range(CC):
                    if c == 0:
                        pool.wait_ge(swap_in[a], 32 * (g + 1))
                    for row, f in ((qk[par][:, a, c, :], 0), (swapped[:, a, c, :], 1)):
                        pool.tensor_tensor(row, row, table[par][:, f, :], ALU.mult).then_inc(turned, 1)

        def rope(eng, g, par, a):
            eng.wait_ge(turned, 2 * CC * (2 * g + a + 1))
            eng.tensor_tensor(qk[par][:, a, :, :], qk[par][:, a, :, :], swapped[:, a, :, :],
                              ALU.add).then_inc(rope_ready, 1)

        def high(act, g, par, a):
            act.wait_ge(rope_ready, 2 * g + a + 1)
            if some(16 * PARTS * g):
                act.wait_ge(sent[a], 16 * PARTS * g)
            act.activation(part[a][0], qk[par][:, a, :, :], ACT.Copy).then_inc(high_ready, 1)

        def rest(eng, g, par, a):
            eng.wait_ge(high_ready, 2 * g + a + 1)
            eng.tensor_tensor(qk[par][:, a, :, :], qk[par][:, a, :, :], part[a][0], ALU.subtract).then_inc(rest_ready, 1)

        def mid(act, g, par, a):
            act.wait_ge(rest_ready, 2 * g + a + 1)
            act.activation(part[a][1], qk[par][:, a, :, :], ACT.Copy).then_inc(mid_ready, 1)

        def low(eng, g, par, a):
            eng.wait_ge(mid_ready, 2 * g + a + 1)
            eng.tensor_tensor(part[a][2], qk[par][:, a, :, :], part[a][1], ALU.subtract).then_inc(low_ready, 1)

        def send(sp, g, a):
            sp.wait_ge(low_ready, 2 * g + a + 1)
            for s in range(PARTS):
                sp.dma_start(split_dram[a, s, :, bass.ds(g * W, W)].rearrange("(c p) n -> p c n", p=P),
                             part[a][s]).then_inc(sent[a], 16)

        def load_stacks(sp, row, col, par):
            for n, pair in enumerate(PAIRS):
                for side in range(2):
                    src = split_dram[side, pair[side], bass.ds(row, D), bass.ds(col, N)]
                    sp.dma_start(stack_a[n * D:(n + 1) * D, par, side, :], src).then_inc(a_loaded, 16)

        with ExitStack() as on:
            even_qk = sb("even_qk", [P, 2, CC, W], F32, on)
            even_table = sb("even_table", [P, 2, W], F32, on)
            qk = [even_qk[:], odd_qk]
            table = [even_table[:], odd_table]
            ps_t = [ps(f"a_ps_t{c}", [P, W], F32, on) for c in range(CC)]
            ps_q = [ps(f"a_ps_q{c}", [P, W], F32, on) for c in range(2 * CC)]
            ps_v = [ps(f"a_ps_v{c}", [P, 2 * C], F32, on) for c in range(2)]
            xn_ready = sem("a_xn_ready", on)
            t_ready = sem("a_t_ready", on)
            xnt_ready = sem("a_xnt_ready", on)
            q_ready = sem("q_ready", on)
            qk_ready = sem("qk_ready", on)
            v_ready = sem("a_v_ready", on)
            v_kept = sem("v_kept", on)
            var_ready = sem("a_var_ready", on)
            root_ready = sem("a_root_ready", on)
            ln_ready = sem("a_ln_ready", on)
            chain = sem("a_chain", on)

            def last_step(i, j):
                return isinstance(i, int) and i == B - 1 and j == GB - 1

            def first_step(i, j):
                return isinstance(i, int) and i == 0 and j == 0

            with nc.Block() as block:
                @block.sync
                def _(sp):
                    def load_table(g, j):
                        used = snap(sp, 4 * CC * (g - 1))
                        if some(used):
                            sp.wait_ge(turned, used)
                        for f, src in enumerate((cos, sin)):
                            sp.dma_start(table[j % 2][:, f, :], src[:, j * W:(j + 1) * W]).then_inc(tab_loaded[j % 2], 16)

                    def swap(g, par, a):
                        made, used = snap(sp, CC * (2 * g + a + 1)), snap(sp, 2 * (g - 1) + a + 1)
                        sp.wait_ge(qk_ready, made)
                        if some(used):
                            sp.wait_ge(rope_ready, used)
                        for odd in range(2):
                            sp.dma_start(swapped[odd::2, a, :, :], qk[par][1 - odd::2, a, :, :]).then_inc(swap_in[a], 16)

                    def batch(i):
                        for j in range(GB):
                            g = i * GB + j
                            for a in range(2):
                                swap(g, j % 2, a)
                            if not last_step(i, j):
                                load_table(g + 1, (j + 1) % GB)
                            if last_step(i, j):
                                for a in range(2):
                                    sp.wait_ge(sent[a], 16 * PARTS * GB)
                                sp.wait_ge(t_ready, CC * G)
                                load_stacks(sp, 0, 0, 0)
                            if not first_step(i, j):
                                for a in range(2):
                                    send(sp, g - 1, a)

                    load_table(0, 0)
                    looped(sp, B, batch)

                @block.tensor
                def _(pe):
                    def turn(g, par):
                        pe.wait_ge(xn_ready, g + 1)
                        if some(CC * g):
                            pe.wait_ge(xnt_ready, CC * g)
                        for c in range(CC):
                            for t in range(GT):
                                ins = pe.transpose(ps_t[c][:, t * P:(t + 1) * P],
                                                   xn[:, par, t, c * P:(c + 1) * P], ident[:])
                            ins.then_inc(t_ready, 1)

                    def batch(i):
                        for j in range(GB):
                            g, par = i * GB + j, j % 2
                            pe.wait_ge(xnt_ready, CC * (g + 1))
                            for m in range(2 * CC):
                                if some(2 * CC * (g - 1) + m + 1):
                                    pe.wait_ge(qk_ready, 2 * CC * (g - 1) + m + 1)
                                for c in range(CC):
                                    ins = pe.matmul(ps_q[m][:], w_qkv[:, c, m * P:(m + 1) * P], xnt[:, par, c, :],
                                                    start=(c == 0), stop=(c == CC - 1))
                                ins.then_inc(q_ready, 1)
                                if m == CC - 1 and not last_step(i, j):
                                    turn(g + 1, 1 - par)
                            for pair in range(2):
                                if some(2 * g + pair - 1):
                                    pe.wait_ge(v_kept, 2 * g + pair - 1)
                                for t in range(2 * pair, 2 * pair + 2):
                                    for c in range(CC):
                                        ins = pe.matmul(ps_v[pair][:, (t % 2) * C:(t % 2 + 1) * C],
                                                        xnt[:, par, c, t * P:(t + 1) * P], w_qkv[:, c, 2 * C:3 * C],
                                                        start=(c == 0), stop=(c == CC - 1))
                                ins.then_inc(v_ready, 1)

                    turn(0, 0)
                    looped(pe, B, batch)

                @block.scalar
                def _(act):
                    def normalize(g, par):
                        if some(CC * (g - 1)):
                            act.wait_ge(t_ready, CC * (g - 1))
                        for t in range(GT):
                            tile = g * GT + t
                            ins = act.activation(xn[:, par, t:t + 1, :], x_all[:, bass.ds(tile, 1), :], ACT.Identity,
                                                 bias=shift[:, bass.ds(tile, 1)], scale=rstd[:, bass.ds(tile, 1)])
                        ins.then_inc(xn_ready, 1)

                    def take(g, par, a):
                        if some(2 * (g - 2) + a + 1):
                            act.wait_ge(low_ready, 2 * (g - 2) + a + 1)
                        for c in range(CC):
                            m = a * CC + c
                            act.wait_ge(q_ready, 2 * CC * g + m + 1)
                            act.activation(qk[par][:, a, c, :], ps_q[m][:], ACT.Identity,
                                           bias=b_qk[:, m:m + 1]).then_inc(qk_ready, 1)

                    def batch(i):
                        for j in range(GB):
                            g, par = i * GB + j, j % 2
                            for a in range(2):
                                take(g, par, a)
                                if not first_step(i, j):
                                    high(act, g - 1, 1 - par, a)
                            if not (isinstance(i, int) and i == B - 1 and j >= GB - 2):
                                if j == GB - 2:
                                    act.wait_ge(ln_ready, 1)
                                normalize(g + 2, par)
                            if not first_step(i, j):
                                for a in range(2):
                                    mid(act, g - 1, 1 - par, a)

                    normalize(0, 0)
                    normalize(1, 1)
                    take_root(act, FIRST, TB, var_ready, root_ready, 0)
                    looped(act, B, batch)

                @block.gpsimd
                def _(pool):
                    def batch(i):
                        for j in range(GB):
                            if not first_step(i, j):
                                before = (j - 1) % GB
                                n = i * GB + j - 1
                                n_before = i * (GB // 2) + (before // 2 if j else -1)
                                rope_products(pool, n, before, n_before)

                    looped(pool, B, batch)

                @block.vector
                def _(dve):
                    def take_turned(g, par):
                        if some(2 * (g - 1)):
                            dve.wait_ge(v_ready, 2 * (g - 1))
                        for c in range(CC):
                            dve.wait_ge(t_ready, CC * g + c + 1)
                            dve.tensor_copy(xnt[:, par, c, :], ps_t[c][:]).then_inc(xnt_ready, 1)

                    def keep_v(g, pair):
                        dve.wait_ge(v_ready, 2 * g + pair + 1)
                        for t in range(2):
                            tile = g * GT + 2 * pair + t
                            ins = dve.tensor_tensor(v_all[:, bass.ds(tile, 1), :].rearrange("p t c -> p (t c)"),
                                                    ps_v[pair][:, t * C:(t + 1) * C], b_v[:], ALU.add)
                        ins.then_inc(v_kept, 1)

                    def batch(i):
                        for j in range(GB):
                            g, par = i * GB + j, j % 2
                            if not first_step(i, j):
                                for a in range(2):
                                    rope(dve, g - 1, 1 - par, a)
                            if not last_step(i, j):
                                take_turned(g + 1, 1 - par)
                            if not first_step(i, j):
                                for a in range(2):
                                    rest(dve, g - 1, 1 - par, a)
                            for a in range(2):
                                keep_v(g, a)
                                if not first_step(i, j):
                                    low(dve, g - 1, 1 - par, a)

                    var_plus_eps(dve, FIRST, TB, chain, 0, var_ready)
                    take_turned(0, 0)
                    rstd_and_shift(dve, FIRST, TB, chain, 0, root_ready, 0, ln_ready)
                    looped(dve, B, batch)
                    dve.wait_ge(v_kept, 2 * G)

        with ExitStack() as on:
            LEAD = TB + 6
            SLOTS = HEADS * TB
            VW = 2 * D
            v_h = sb("v_h", [P, 2, TB, VW], F32, on)
            half_max = sb("half_max", [P, 2, TB, 2], F32, on)
            neg_max = sb("neg_max", [P, TB], F32, on)
            max_part = sb("max_part", [P, PARTS, TB], BF16, on)
            max_rows = sb("max_rows", [PARTS * TB, P], BF16, on)
            o_t = sb("o_t", [P, W], F32, on)
            recip = sb("recip", [P, NJ, NJ], F32, on)
            ps_e = [ps(f"ps_e{n}", [P, W], F32, on) for n in range(2)]
            ps_m = [ps(f"ps_m{n}", [P, 2, W], F32, on) for n in range(2)]
            ps_o = ps("ps_o", [P, W], F32, on)
            ps_x = ps("ps_x", [P, W], F32, on)

            def spare(kt):
                return kt % TB not in (3, 4, 5, 6, 13)

            def e_bank(kt, j):
                return ps_x if j == NJ - 1 and spare(kt) else ps_e[j % 2]

            def head_slice(h):
                return v_all[:, bass.ds(h // H * TB, TB), bass.ds(h % H * D, D)]

            ones_ready = sem("ones_ready", on)
            b_loaded = sem("b_loaded", on)
            m_loaded = sem("m_loaded", on)
            v_copied = sem("v_copied", on)
            e_ready = sem("e_ready", on)
            exp_done = sem("exp_done", on)
            s_ready = sem("s_ready", on)
            max_done = sem("max_done", on)
            split = sem("split", on)
            rows_ready = sem("rows_ready", on)
            rows_taken = sem("rows_taken", on)
            pv_done = sem("pv_done", on)
            o_taken = sem("o_taken", on)
            o_turned = sem("o_turned", on)
            recip_done = sem("recip_done", on)
            o_kept = sem("o_kept", on)
            bias_added = sem("bias_added", on)

            with nc.Block() as block:
                @block.sync
                def _(sp):
                    def load_a(h, par):
                        row, col = h % H * D, h // H * N
                        row, col = snap(sp, row), snap(sp, col)
                        made, copied = snap(sp, 2 * TB * (h - 1)), snap(sp, 32 * (h - 1))
                        if some(made):
                            sp.wait_ge(s_ready, made)
                        if some(copied):
                            sp.wait_ge(b_loaded, copied)
                        load_stacks(sp, row, col, par)

                    def copy_b(h, par):
                        loaded, copied = snap(sp, 32 * len(PAIRS) * (h + 1)), snap(sp, 32 * h)
                        used = snap(sp, NJ * TB * (h - 1))
                        sp.wait_ge(a_loaded, loaded)
                        if some(copied):
                            sp.wait_ge(b_loaded, copied)
                        if some(used):
                            sp.wait_ge(e_ready, used)
                        sp.dma_start(q_b[0:R, par, :], stack_a[0:R, par, 0, :]).then_inc(b_loaded, 16)
                        sp.dma_start(k_b[0:R, par, :], stack_a[0:R, par, 1, :]).then_inc(b_loaded, 16)

                    def load_max(h, par):
                        sp.wait_ge(rows_taken, h + 1)
                        sp.dma_start(q_b[R:R + PARTS, par, :], max_rows[:]).then_inc(m_loaded, 16)

                    def two_heads(i):
                        for e in range(2):
                            h = 2 * i + e + 1
                            if isinstance(i, int) and h >= HEADS:
                                continue
                            copy_b(h, (e + 1) % 2)
                            if not (isinstance(i, int) and h + 1 >= HEADS):
                                load_a(h + 1, e)
                            load_max(h, (e + 1) % 2)

                    sp.wait_ge(a_loaded, 32 * len(PAIRS))
                    load_a(1, 1)
                    for a in range(2):
                        send(sp, G - 1, a)
                    for a in range(2):
                        sp.wait_ge(sent[a], 16 * PARTS * G)
                    copy_b(0, 0)
                    load_max(0, 0)
                    looped(sp, HEADS // 2, two_heads)

                @block.gpsimd
                def _(pool):
                    rope_products(pool, G - 1, GB - 1, G // 2 - 1)
                    for split_step in (rope, rest, low):
                        for a in range(2):
                            split_step(pool, G - 1, 1, a)
                    pool.wait_ge(rope_ready, 2 * G)
                    pool.memset(v_h[:], 1.0).then_inc(ones_ready, 1)
                    pool.wait_ge(ones_ready, 1)
                    pool.memset(k_b[R:R + PARTS, :, :], 1.0).then_inc(ones_ready, 1)
                    pool.wait_ge(ones_ready, 2)

                    def two_heads(i):
                        for e in range(2):
                            h = 2 * i + e
                            if some(TB * (h - 1)):
                                pool.wait_ge(pv_done, TB * (h - 1))
                            pool.tensor_copy(v_h[:, e, :, 0:D], head_slice(h)).then_inc(v_copied, 1)
                            here = x_all[:, bass.ds(h * (T // HEADS), T // HEADS), :]
                            pool.tensor_tensor(here, here, b_proj[:].rearrange("p (o c) -> p o c", o=1)
                                               .broadcast_to([P, T // HEADS, C]), ALU.add).then_inc(bias_added, 1)

                    looped(pool, HEADS // 2, two_heads)
                    pool.wait_ge(bias_added, HEADS)

                @block.tensor
                def _(pe):
                    def score_max(m, j, par, t):
                        if j % 2 == 0:
                            if some(2 * m + j // 2 - 1):
                                pe.wait_ge(max_done, 2 * m + j // 2 - 1)
                        ins = pe.matmul(ps_m[j // 2][:, j % 2, :], stack_a[0:R, par, 0, t * P:(t + 1) * P],
                                        stack_a[0:R, par, 1, j * W:(j + 1) * W], start=True, stop=True)
                        if j % 2 == 1:
                            ins.then_inc(s_ready, 1)

                    def turn_max(h):
                        pe.wait_ge(split, 5 * (h + 1))
                        if some(h - 1):
                            pe.wait_ge(o_kept, h - 1)
                        pe.matmul(ps_x[0:PARTS * TB, 0:P], max_part[:].rearrange("p s t -> p (s t)"), ident_b[:],
                                  start=True, stop=True).then_inc(rows_ready, 1)

                    def turn_out(h):
                        pe.wait_ge(o_taken, 2 * (h + 1))
                        pe.wait_ge(rows_taken, h + 2)
                        for s in range(W // P):
                            ins = pe.transpose(ps_x[:, s * P:(s + 1) * P], o_t[:, s * P:(s + 1) * P], ident[:])
                        ins.then_inc(o_turned, 1)

                    def pv(k, par, kt):
                        pe.wait_ge(exp_done, NJ * (k + 1))
                        for j in range(NJ):
                            ins = pe.matmul(ps_o[VW * j:VW * (j + 1), :], v_h[:, par, kt, :],
                                            probs[:, kt % 2, j * W:(j + 1) * W], start=(kt == 0), stop=(kt == TB - 1))
                        ins.then_inc(pv_done, 1)

                    def pv_before(k, h, e, kt):
                        if isinstance(k, int) and k == 0:
                            return
                        if kt == 1:
                            pe.wait_ge(v_copied, h + 1)
                            if some(2 * h):
                                pe.wait_ge(o_taken, 2 * h)
                        if kt == 0:
                            pv(k - 1, 1 - e, TB - 1)
                        else:
                            pv(k - 1, e, kt - 1)

                    def last_in_bank(kt, j):
                        before = j - 1
                        while e_bank(kt + before // NJ, before % NJ) is not e_bank(kt, j):
                            before -= 1
                        return before

                    def two_heads(i):
                        for s in range(2 * TB):
                            e, kt = s // TB, s % TB
                            k = i * (2 * TB) + s
                            h = 2 * i + e
                            m = k + LEAD
                            ahead = (s + LEAD) // TB % 2
                            has_max = not (isinstance(i, int) and m >= SLOTS)
                            if kt == 0:
                                pe.wait_ge(b_loaded, 32 * (h + 1))
                                pe.wait_ge(m_loaded, 16 * (h + 1))
                            if has_max and (s + LEAD) % TB == 0:
                                pe.wait_ge(a_loaded, 32 * len(PAIRS) * (2 * i + (s + LEAD) // TB + 1))
                            for j0 in range(0, NJ, 2):
                                for j in (j0, j0 + 1):
                                    before = last_in_bank(kt, j)
                                    if some(NJ * k + before + 1):
                                        pe.wait_ge(exp_done, NJ * k + before + 1)
                                    if j == NJ - 1 and kt == 7 and not (isinstance(i, int) and h == 0):
                                        pe.wait_ge(o_kept, h)
                                    if j == NJ - 1 and kt == 14 and not (isinstance(i, int) and h + 1 >= HEADS):
                                        pe.wait_ge(rows_taken, h + 2)
                                    pe.matmul(e_bank(kt, j)[:], k_b[0:R + PARTS, e, kt * P:(kt + 1) * P],
                                              q_b[0:R + PARTS, e, j * W:(j + 1) * W], start=True, stop=True).then_inc(e_ready, 1)
                                if has_max and j0 == 0:
                                    for j in range(NJ):
                                        score_max(m, j, ahead, (s + LEAD) % TB)
                                if not has_max and j0 == 0:
                                    pv_before(k, h, e, kt)
                            if kt == 3 and not (isinstance(i, int) and h == 0):
                                turn_out(h - 1)
                            if kt == 13 and not (isinstance(i, int) and h + 1 >= HEADS):
                                turn_max(h + 1)
                            if has_max:
                                pv_before(k, h, e, kt)

                    for m in range(LEAD):
                        if m % TB == 0:
                            pe.wait_ge(a_loaded, 32 * len(PAIRS) * (m // TB + 1))
                        for j in range(NJ):
                            score_max(m, j, m // TB, m % TB)
                    turn_max(0)
                    pe.wait_ge(ones_ready, 2)
                    looped(pe, HEADS // 2, two_heads)
                    pv(SLOTS - 1, 1, TB - 1)
                    pe.wait_ge(o_taken, 2 * HEADS)
                    pe.wait_ge(o_kept, HEADS - 1)
                    for s in range(W // P):
                        ins = pe.transpose(ps_x[:, s * P:(s + 1) * P], o_t[:, s * P:(s + 1) * P], ident[:])
                    ins.then_inc(o_turned, 1)

                @block.scalar
                def _(act):
                    def take_rows(h):
                        act.wait_ge(rows_ready, h + 1)
                        if some(16 * h):
                            act.wait_ge(m_loaded, 16 * h)
                        act.activation(max_rows[:], ps_x[0:PARTS * TB, 0:P], ACT.Copy).then_inc(rows_taken, 1)

                    def take_out(h, half):
                        act.wait_ge(pv_done, TB * (h + 1))
                        if some(h):
                            act.wait_ge(o_turned, h)
                        cols = slice(half * W // 2, (half + 1) * W // 2)
                        act.activation(o_t[:, cols], ps_o[:, cols], ACT.Copy).then_inc(o_taken, 1)

                    def two_heads(i):
                        for s in range(2 * TB):
                            e, kt = s // TB, s % TB
                            k = i * (2 * TB) + s
                            h = 2 * i + e
                            for j in range(NJ):
                                act.wait_ge(e_ready, NJ * k + j + 1)
                                if j == 0:
                                    if some(k - 1):
                                        act.wait_ge(pv_done, k - 1)
                                act.activation(probs[:, kt % 2, j * W:(j + 1) * W], e_bank(kt, j)[:], ACT.Exp,
                                               scale=scale).then_inc(exp_done, 1)
                                if j % 2 and kt == 1 - j // 2 and not (isinstance(i, int) and h == 0):
                                    take_out(h - 1, 1 - j // 2)
                            if kt == 13 and not (isinstance(i, int) and h + 1 >= HEADS):
                                take_rows(h + 1)

                    for split_step in (high, mid):
                        for a in range(2):
                            split_step(act, G - 1, 1, a)
                    take_rows(0)
                    looped(act, HEADS // 2, two_heads)
                    for half in range(2):
                        take_out(HEADS - 1, half)

                @block.vector
                def _(dve):
                    def slot_max(m, par, t):
                        for half in range(2):
                            dve.wait_ge(s_ready, 2 * m + half + 1)
                            dve.tensor_reduce(half_max[:, par, t, half:half + 1], ps_m[half][:], AX.XY,
                                              ALU.max).then_inc(max_done, 1)

                    def negate(h, par):
                        dve.wait_ge(max_done, 2 * TB * (h + 1))
                        dve.tensor_reduce(neg_max[:], half_max[:, par, :, :], AX.X, ALU.max,
                                          negate=True).then_inc(split, 1)

                    def part_of_max(h, s):
                        if s == 0 and some(h):
                            dve.wait_ge(rows_ready, h)
                        dve.wait_ge(split, 5 * h + 2 * s + 1)
                        dve.tensor_copy(max_part[:, s, :], neg_max[:]).then_inc(split, 1)
                        dve.wait_ge(split, 5 * h + 2 * s + 2)
                        rest = neg_max[:] if s < PARTS - 2 else max_part[:, PARTS - 1, :]
                        dve.tensor_tensor(rest, neg_max[:], max_part[:, s, :], ALU.subtract).then_inc(split, 1)

                    turned = ps_x[:].rearrange("p (s j d) -> p s j d", j=NJ, d=VW)

                    def invert_sums(h):
                        dve.wait_ge(o_turned, h + 1)
                        if some(h):
                            dve.wait_ge(o_kept, h)
                        dve.reciprocal(recip[:], turned[:, :, :, D]).then_inc(recip_done, 1)

                    def keep_out(h):
                        dve.wait_ge(recip_done, h + 1)
                        dst = head_slice(h).rearrange("p (j s) d -> p s j d", j=NJ)
                        dve.tensor_tensor(dst, turned[:, :, :, 0:D],
                                          recip[:].rearrange("p s (j o) -> p s j o", o=1).broadcast_to([P, NJ, NJ, D]),
                                          ALU.mult).then_inc(o_kept, 1)

                    def two_heads(i):
                        for s in range(2 * TB):
                            e, kt = s // TB, s % TB
                            k = i * (2 * TB) + s
                            h = 2 * i + e
                            if not (isinstance(i, int) and k + LEAD >= SLOTS):
                                slot_max(k + LEAD, (s + LEAD) // TB % 2, (s + LEAD) % TB)
                            if not (isinstance(i, int) and h + 1 >= HEADS):
                                if kt == 9:
                                    negate(h + 1, 1 - e)
                                if kt in (10, 11):
                                    part_of_max(h + 1, kt - 10)
                            if not (isinstance(i, int) and h == 0):
                                if kt == 4:
                                    invert_sums(h - 1)
                                if kt == 5:
                                    keep_out(h - 1)

                    for m in range(LEAD):
                        slot_max(m, m // TB, m % TB)
                        if m == TB - 1:
                            negate(0, 0)
                            for s in range(PARTS - 1):
                                part_of_max(0, s)
                    looped(dve, HEADS // 2, two_heads)
                    invert_sums(HEADS - 1)
                    keep_out(HEADS - 1)
                    dve.wait_ge(o_kept, HEADS)

        both.close()

        with ExitStack() as on:
            attn = sb("attn", [P, 2, GT, C], F32, on)
            attn_t = sb("attn_t", [P, 2, CC, W], F32, on)
            ps_t = [ps(f"p_ps_t{c}", [P, W], F32, on) for c in range(2 * CC)]
            ps_y = [ps(f"p_ps_y{c}", [P, 2, C], F32, on) for c in range(2)]
            attn_ready = sem("attn_ready", on)
            t_ready = sem("p_t_ready", on)
            attn_t_ready = sem("attn_t_ready", on)
            y_ready = sem("y_ready", on)
            sum_ready = sem("sum_ready", on)
            counted = sem("p_counted", on)
            var_ready = sem("p_var_ready", on)
            root_ready = sem("p_root_ready", on)
            ln_ready = sem("p_ln_ready", on)
            chain = sem("p_chain", on)

            with nc.Block() as block:
                @block.gpsimd
                def _(pool):
                    def batch(i):
                        for j in range(GB):
                            g = i * GB + j
                            if isinstance(g, int) and g == 0:
                                continue
                            if some(CC * (g - 1)):
                                pool.wait_ge(t_ready, CC * (g - 1))
                            pool.tensor_copy(attn[:, j % 2, :, :], v_all[:, bass.ds(g * GT, GT), :]).then_inc(attn_ready, 1)

                    looped(pool, B, batch)

                @block.tensor
                def _(pe):
                    def turn(g, par):
                        if some(g):
                            pe.wait_ge(attn_ready, g)
                        src = attn[:, par, :, :] if some(g) else v_all[:, 0:GT, :]
                        if some(CC * (g - 1)):
                            pe.wait_ge(attn_t_ready, CC * (g - 1))
                        for c in range(CC):
                            for t in range(GT):
                                ins = pe.transpose(ps_t[par * CC + c][:, t * P:(t + 1) * P],
                                                   src[:, t, c * P:(c + 1) * P], ident[:])
                            ins.then_inc(t_ready, 1)

                    def batch(i):
                        for j in range(GB):
                            g, par = i * GB + j, j % 2
                            if not (isinstance(i, int) and i == B - 1 and j == GB - 1):
                                turn(g + 1, 1 - par)
                            pe.wait_ge(attn_t_ready, CC * (g + 1))
                            for pair in range(2):
                                if some(2 * g + pair - 1):
                                    pe.wait_ge(sum_ready, 2 * g + pair - 1)
                                for t in range(2 * pair, 2 * pair + 2):
                                    for c in range(CC):
                                        ins = pe.matmul(ps_y[pair][:, t % 2, :], attn_t[:, par, c, t * P:(t + 1) * P],
                                                        w_proj[:, c, :], start=(c == 0), stop=(c == CC - 1))
                                ins.then_inc(y_ready, 1)

                    turn(0, 0)
                    looped(pe, B, batch)

                @block.scalar
                def _(act):
                    def batch(i):
                        for j in range(GB):
                            g, par = i * GB + j, j % 2
                            if some(2 * (g - 1)):
                                act.wait_ge(y_ready, 2 * (g - 1))
                            for c in range(CC):
                                act.wait_ge(t_ready, CC * g + c + 1)
                                act.activation(attn_t[:, par, c, :], ps_t[par * CC + c][:],
                                               ACT.Copy).then_inc(attn_t_ready, 1)
                            if isinstance(i, int) and i == B - 1 and j == 1:
                                take_root(act, 0, FIRST, var_ready, root_ready, 0)

                    looped(act, B, batch)

                @block.vector
                def _(dve):
                    def batch(i):
                        for n0 in range(2 * GB):
                            n, pair = i * 2 * GB + n0, n0 % 2
                            here = x_all[:, bass.ds(2 * n, 2), :]
                            dve.wait_ge(y_ready, n + 1)
                            dve.tensor_tensor(here, here, ps_y[pair][:], ALU.add).then_inc(sum_ready, 1)
                            dve.wait_ge(sum_ready, n + 1)
                            for t in range(2):
                                dve.bn_stats(stats[:, bass.ds(2 * n + t, 1), :],
                                             x_all[:, bass.ds(2 * n + t, 1), :]).then_inc(counted, 1)
                            if isinstance(i, int) and i == B - 1 and n0 == 1:
                                dve.wait_ge(counted, FIRST)
                                var_plus_eps(dve, 0, FIRST, chain, 0, var_ready)
                            if isinstance(i, int) and i == B - 1 and n0 == 4:
                                rstd_and_shift(dve, 0, FIRST, chain, 0, root_ready, 0, ln_ready)

                    looped(dve, B, batch)
                    dve.wait_ge(counted, T)
                    dve.wait_ge(ln_ready, 1)

        ffn("ffn2", True)


def kernel(L0_attn_x, L0_attn_qkv_w, L0_attn_qkv_b, L0_attn_proj_w, L0_attn_proj_b, L0_ffn_W_r, L0_ffn_W_k,
           L0_ffn_W_v, L0_ffn_mu_r, L0_ffn_mu_k):
    import numpy as np
    import concourse.bacc as bacc
    from concourse.bass_utils import run_bass_kernel_spmd

    B, N, C = L0_attn_x.shape
    D = C // 16
    inv = np.float32(1.0) / np.float32(10000.0) ** (np.arange(0, D, 2, dtype=np.float32) / np.float32(D))
    angle = np.arange(N, dtype=np.float32)[None, :] * inv.astype(np.float32)[:, None]
    rows = (np.arange(P) % D) // 2
    sign = np.where(np.arange(P) % 2 == 0, -1.0, 1.0).astype(np.float32)[:, None]

    def columns(v):
        return np.asarray(v).reshape(-1, P).T

    arrays = {
        "x": L0_attn_x, "wr_t": L0_ffn_W_r.T, "wk_t": L0_ffn_W_k.T, "wv_t": L0_ffn_W_v.T,
        "mu_r": columns(L0_ffn_mu_r), "mu_k": columns(L0_ffn_mu_k),
        "qkv_t": L0_attn_qkv_w.T, "qk_b": columns(L0_attn_qkv_b[:2 * C]), "qkv_b": L0_attn_qkv_b,
        "proj_t": L0_attn_proj_w.T, "proj_b": L0_attn_proj_b,
        "cos": np.cos(angle)[rows], "sin": np.sin(angle)[rows] * sign,
    }
    arrays = {f"in_{k}": np.ascontiguousarray(np.asarray(v)) for k, v in arrays.items()}
    nc = bacc.Bacc("TRN2", target_bir_lowering=False, num_devices=1)
    args = [nc.dram_tensor(k, v.shape, F32, kind="ExternalInput").ap() for k, v in arrays.items()]
    out = nc.dram_tensor("out_0", (B, N, C), F32, kind="ExternalOutput").ap()
    macaron(nc, *args, out)
    r = run_bass_kernel_spmd(nc, [arrays], core_ids=[0])
    return r.results[0]["out_0"]
```
